# Optimizing a Trainium2 kernel written in Bass

```python
import numpy as np
import jax
import jax.numpy as jnp

def _softmax(x, axis=-1):
    return jax.nn.softmax(x, axis=axis)

def _gelu(x):
    return jax.nn.gelu(x, approximate=True)

def _silu(x):
    return jax.nn.silu(x)

def _sigmoid(x):
    return jax.nn.sigmoid(x)

def _layernorm(x, axis=-1, eps=1e-05):
    m = jnp.mean(x, axis=axis, keepdims=True)
    v = jnp.var(x, axis=axis, keepdims=True)
    return (x - m) / jnp.sqrt(v + eps)

def _scatter_add(tgt, idx, src, axis=0):
    return tgt.at[idx].add(src)

def _segment_sum(src, seg, n):
    return jax.ops.segment_sum(src, seg, n)
kernel_name = 'mk_adaln_d2_jaxref_r4_a226e6'

def setup_inputs(seed: int=0):
    np.random.seed(seed)
    _w = jnp.asarray

    def _L0_attn_setup():
        import jax, jax.numpy as jnp
        import numpy as np
        B, T, D = (2, 512, 256)
        H = 16
        DH = D // H

        def alibi_bias(n_heads, token_cnt, dtype=jnp.float32):
            slopes = 2.0 ** (-8.0 * jnp.arange(1, n_heads + 1, dtype=dtype) / n_heads)
            pos = jnp.arange(token_cnt, dtype=dtype)
            rel = pos[None, :] - pos[:, None]
            return slopes[:, None, None] * rel[None, :, :]
        key = jax.random.key(seed)
        ks = jax.random.split(key, 5)
        s = 1.0 / np.sqrt(D)
        return {'x': jax.random.normal(ks[0], (B, T, D), dtype=jnp.float32), 'W_query': jax.random.normal(ks[1], (D, D), dtype=jnp.float32) * s, 'W_key': jax.random.normal(ks[2], (D, D), dtype=jnp.float32) * s, 'W_value': jax.random.normal(ks[3], (D, D), dtype=jnp.float32) * s, 'W_proj': jax.random.normal(ks[4], (D, D), dtype=jnp.float32) * s, 'b_proj': jnp.zeros((D,), dtype=jnp.float32)}
    _L0_attn_in = _L0_attn_setup()

    def _L0_ffn_setup():
        import jax, jax.numpy as jnp
        import numpy as np
        DIM = 256

        def _reference_tuple_inner(x, W_r, W_k, W_v, mu_r, mu_k):
            B, T, C = x.shape
            x_prev = jnp.concatenate([jnp.zeros((B, 1, C), x.dtype), x[:, :-1, :]], axis=1)
            xr = mu_r * x + (1.0 - mu_r) * x_prev
            xk = mu_k * x + (1.0 - mu_k) * x_prev
            r = jax.nn.sigmoid(jnp.einsum('btc,dc->btd', xr, W_r))
            k = jnp.einsum('btc,dc->btd', xk, W_k)
            k_act = jnp.square(jax.nn.relu(k))
            out = r * jnp.einsum('btc,dc->btd', k_act, W_v)
            new_state = x[:, -1, :]
            return (out, new_state)
        key = jax.random.key(seed)
        ks = jax.random.split(key, 6)
        B, T, C = (8, 512, DIM)
        x = jax.random.normal(ks[0], (B, T, C), dtype=jnp.float32)
        s = 1.0 / np.sqrt(C)
        W_r = jax.random.uniform(ks[1], (C, C), jnp.float32, -s, s)
        W_k = jax.random.uniform(ks[2], (C, C), jnp.float32, -s, s)
        W_v = jax.random.uniform(ks[3], (C, C), jnp.float32, -s, s)
        mu_r = jax.random.uniform(ks[4], (C,), jnp.float32)
        mu_k = jax.random.uniform(ks[5], (C,), jnp.float32)
        return {'x': x, 'W_r': W_r, 'W_k': W_k, 'W_v': W_v, 'mu_r': mu_r, 'mu_k': mu_k}
    _L0_ffn_in = _L0_ffn_setup()
    _L0_c = _w((lambda *s: np.random.randn(*s).astype(np.float32) * 0.05)(8, 256))
    _L0_wmod = _w((lambda *s: np.random.randn(*s).astype(np.float32) * 0.05)(256, 6 * 256) * 256 ** (-0.5))

    def _L1_attn_setup():
        import jax, jax.numpy as jnp
        import numpy as np
        MODEL_DIM = 256
        NUM_HEADS = 16
        HEAD_DIM = MODEL_DIM // NUM_HEADS
        ROPE_PERIOD = 10000.0

        def _rope_cos_sin(seq_len, dim, dtype):
            inv_freq = 1.0 / ROPE_PERIOD ** (jnp.arange(0, dim, 2, dtype=jnp.float32) / dim)
            t = jnp.arange(seq_len, dtype=jnp.float32)
            freqs = jnp.outer(t, inv_freq)
            emb = jnp.concatenate([freqs, freqs], axis=-1)
            return (jnp.cos(emb).astype(dtype), jnp.sin(emb).astype(dtype))

        def _rope_embed(x):
            S, D = (x.shape[-2], x.shape[-1])
            cos, sin = _rope_cos_sin(S, D, x.dtype)
            x1 = x[..., :D // 2]
            x2 = x[..., D // 2:]
            rotated = jnp.concatenate([-x2, x1], axis=-1)
            return x * cos + rotated * sin
        key = jax.random.key(seed)
        kx, kq, kk, kv, ko = jax.random.split(key, 5)
        std = 0.02
        return {'x': jax.random.normal(kx, (2, 512, MODEL_DIM), dtype=jnp.float32), 'Wq': std * jax.random.normal(kq, (MODEL_DIM, MODEL_DIM), dtype=jnp.float32), 'Wk': std * jax.random.normal(kk, (MODEL_DIM, MODEL_DIM), dtype=jnp.float32), 'Wv': std * jax.random.normal(kv, (MODEL_DIM, MODEL_DIM), dtype=jnp.float32), 'Wo': std * jax.random.normal(ko, (MODEL_DIM, MODEL_DIM), dtype=jnp.float32)}
    _L1_attn_in = _L1_attn_setup()

    def _L1_ffn_setup():
        import jax, jax.numpy as jnp
        import numpy as np
        ALPHA = 1.0
        key = jax.random.key(seed)
        ks = jax.random.split(key, 7)
        B, S, IN, OUT = (8, 2048, 256, 256)
        RANK, DDIM, UDIM = (4, 100, 50)
        return {'hidden_states': jax.random.normal(ks[0], (B, S, IN), dtype=jnp.float32), 'W': jax.random.normal(ks[1], (OUT, IN), dtype=jnp.float32) * 0.02, 'b': jax.random.normal(ks[2], (OUT,), dtype=jnp.float32) * 0.02, 'lora_down': jax.random.normal(ks[3], (RANK, DDIM), dtype=jnp.float32) * 0.1, 'lora_up': jax.random.normal(ks[4], (UDIM, RANK), dtype=jnp.float32) * 0.1, 'down_aux': jax.random.normal(ks[5], (DDIM, IN), dtype=jnp.float32) * 0.03, 'up_aux': jax.random.normal(ks[6], (OUT, UDIM), dtype=jnp.float32) * 0.03}
    _L1_ffn_in = _L1_ffn_setup()
    _L1_c = _w((lambda *s: np.random.randn(*s).astype(np.float32) * 0.05)(8, 256))
    _L1_wmod = _w((lambda *s: np.random.randn(*s).astype(np.float32) * 0.05)(256, 6 * 256) * 256 ** (-0.5))
    _d = {'L0_attn_x': _L0_attn_in['x'], 'L0_attn_W_query': _L0_attn_in['W_query'], 'L0_attn_W_key': _L0_attn_in['W_key'], 'L0_attn_W_value': _L0_attn_in['W_value'], 'L0_attn_W_proj': _L0_attn_in['W_proj'], 'L0_attn_b_proj': _L0_attn_in['b_proj'], 'L0_ffn_W_r': _L0_ffn_in['W_r'], 'L0_ffn_W_k': _L0_ffn_in['W_k'], 'L0_ffn_W_v': _L0_ffn_in['W_v'], 'L0_ffn_mu_r': _L0_ffn_in['mu_r'], 'L0_ffn_mu_k': _L0_ffn_in['mu_k'], 'L0_c': _L0_c, 'L0_wmod': _L0_wmod, 'L1_attn_Wq': _L1_attn_in['Wq'], 'L1_attn_Wk': _L1_attn_in['Wk'], 'L1_attn_Wv': _L1_attn_in['Wv'], 'L1_attn_Wo': _L1_attn_in['Wo'], 'L1_ffn_W': _L1_ffn_in['W'], 'L1_ffn_b': _L1_ffn_in['b'], 'L1_ffn_lora_down': _L1_ffn_in['lora_down'], 'L1_ffn_lora_up': _L1_ffn_in['lora_up'], 'L1_ffn_down_aux': _L1_ffn_in['down_aux'], 'L1_ffn_up_aux': _L1_ffn_in['up_aux'], 'L1_c': _L1_c, 'L1_wmod': _L1_wmod}
    _x0 = _d['L0_attn_x']
    _d['L0_attn_x'] = jax.random.normal(jax.random.fold_in(jax.random.key(seed), 1), (8, 1024, 256), dtype=_x0.dtype)
    del _x0
    return _d

def reference(L0_attn_x, L0_attn_W_query, L0_attn_W_key, L0_attn_W_value, L0_attn_W_proj, L0_attn_b_proj, L0_ffn_W_r, L0_ffn_W_k, L0_ffn_W_v, L0_ffn_mu_r, L0_ffn_mu_k, L0_c, L0_wmod, L1_attn_Wq, L1_attn_Wk, L1_attn_Wv, L1_attn_Wo, L1_ffn_W, L1_ffn_b, L1_ffn_lora_down, L1_ffn_lora_up, L1_ffn_down_aux, L1_ffn_up_aux, L1_c, L1_wmod):

    def _L0_attn_ref(x, W_query, W_key, W_value, W_proj, b_proj):
        import jax, jax.numpy as jnp
        import numpy as np
        B, T, D = (2, 512, 256)
        H = 16
        DH = D // H

        def alibi_bias(n_heads, token_cnt, dtype=jnp.float32):
            slopes = 2.0 ** (-8.0 * jnp.arange(1, n_heads + 1, dtype=dtype) / n_heads)
            pos = jnp.arange(token_cnt, dtype=dtype)
            rel = pos[None, :] - pos[:, None]
            return slopes[:, None, None] * rel[None, :, :]
        b, t, _ = x.shape

        def heads(y):
            return y.reshape(b, t, H, DH).transpose(0, 2, 1, 3)
        q = heads(x @ W_query)
        k = heads(x @ W_key)
        v = heads(x @ W_value)
        scores = jnp.einsum('bhqd,bhkd->bhqk', q, k)
        causal = jnp.triu(jnp.ones((t, t), dtype=bool), k=1)
        scores = jnp.where(causal[None, None], -jnp.inf, scores)
        scores = scores + alibi_bias(H, t, scores.dtype)[None]
        scores = scores / jnp.sqrt(jnp.asarray(DH, scores.dtype))
        w = jax.nn.softmax(scores, axis=-1)
        ctx = jnp.einsum('bhqk,bhkd->bqhd', w, v).reshape(b, t, H * DH)
        return ctx @ W_proj + b_proj

    def _L0_ffn_ref(x, W_r, W_k, W_v, mu_r, mu_k):
        import jax, jax.numpy as jnp
        import numpy as np
        DIM = 256

        def _reference_tuple_inner(x, W_r, W_k, W_v, mu_r, mu_k):
            B, T, C = x.shape
            x_prev = jnp.concatenate([jnp.zeros((B, 1, C), x.dtype), x[:, :-1, :]], axis=1)
            xr = mu_r * x + (1.0 - mu_r) * x_prev
            xk = mu_k * x + (1.0 - mu_k) * x_prev
            r = jax.nn.sigmoid(jnp.einsum('btc,dc->btd', xr, W_r))
            k = jnp.einsum('btc,dc->btd', xk, W_k)
            k_act = jnp.square(jax.nn.relu(k))
            out = r * jnp.einsum('btc,dc->btd', k_act, W_v)
            new_state = x[:, -1, :]
            return (out, new_state)
        return _reference_tuple_inner(x, W_r, W_k, W_v, mu_r, mu_k)[0]

    def _L1_attn_ref(x, Wq, Wk, Wv, Wo):
        import jax, jax.numpy as jnp
        import numpy as np
        MODEL_DIM = 256
        NUM_HEADS = 16
        HEAD_DIM = MODEL_DIM // NUM_HEADS
        ROPE_PERIOD = 10000.0

        def _rope_cos_sin(seq_len, dim, dtype):
            inv_freq = 1.0 / ROPE_PERIOD ** (jnp.arange(0, dim, 2, dtype=jnp.float32) / dim)
            t = jnp.arange(seq_len, dtype=jnp.float32)
            freqs = jnp.outer(t, inv_freq)
            emb = jnp.concatenate([freqs, freqs], axis=-1)
            return (jnp.cos(emb).astype(dtype), jnp.sin(emb).astype(dtype))

        def _rope_embed(x):
            S, D = (x.shape[-2], x.shape[-1])
            cos, sin = _rope_cos_sin(S, D, x.dtype)
            x1 = x[..., :D // 2]
            x2 = x[..., D // 2:]
            rotated = jnp.concatenate([-x2, x1], axis=-1)
            return x * cos + rotated * sin
        B, S, Dm = x.shape
        H, Dh = (NUM_HEADS, HEAD_DIM)
        q = (x @ Wq.T).reshape(B, S, H, Dh).transpose(0, 2, 1, 3)
        k = (x @ Wk.T).reshape(B, S, H, Dh).transpose(0, 2, 1, 3)
        v = (x @ Wv.T).reshape(B, S, H, Dh).transpose(0, 2, 1, 3)
        q = _rope_embed(q)
        k = _rope_embed(k)
        scores = jnp.einsum('bhqd,bhkd->bhqk', q, k) / jnp.sqrt(jnp.asarray(Dh, x.dtype))
        neg_inf = jnp.finfo(x.dtype).min
        causal = jnp.triu(jnp.full((S, S), neg_inf, dtype=x.dtype), k=1)
        scores = scores + causal
        attn = jax.nn.softmax(scores, axis=-1)
        out = jnp.einsum('bhqk,bhkd->bhqd', attn, v)
        out = out.transpose(0, 2, 1, 3).reshape(B, S, Dm)
        return out @ Wo.T

    def _L1_ffn_ref(hidden_states, W, b, lora_down, lora_up, down_aux, up_aux):
        import jax, jax.numpy as jnp
        import numpy as np
        ALPHA = 1.0
        lilora_weight = up_aux @ (lora_up @ (lora_down @ down_aux))
        base = jnp.einsum('bsi,oi->bso', hidden_states, W) + b
        delta = jnp.einsum('bsi,oi->bso', hidden_states, lilora_weight)
        return base + ALPHA * delta
    x = L0_attn_x
    mod = (_silu(L0_c) @ L0_wmod).reshape(L0_c.shape[0], 6, 1, -1)
    sa, ca, ga, sb, cb, gb = (mod[:, 0], mod[:, 1], mod[:, 2], mod[:, 3], mod[:, 4], mod[:, 5])
    ga = (2 * (ga >= 0) - 1) * jnp.maximum(jnp.abs(ga), 0.25)
    gb = (2 * (gb >= 0) - 1) * jnp.maximum(jnp.abs(gb), 0.25)
    h = _layernorm(x, axis=-1) * (1 + ca) + sa
    x = x + ga * _L0_attn_ref(h, L0_attn_W_query, L0_attn_W_key, L0_attn_W_value, L0_attn_W_proj, L0_attn_b_proj)
    h = _layernorm(x, axis=-1) * (1 + cb) + sb
    x = x + gb * _L0_ffn_ref(h, L0_ffn_W_r, L0_ffn_W_k, L0_ffn_W_v, L0_ffn_mu_r, L0_ffn_mu_k)
    mod = (_silu(L1_c) @ L1_wmod).reshape(L1_c.shape[0], 6, 1, -1)
    sa, ca, ga, sb, cb, gb = (mod[:, 0], mod[:, 1], mod[:, 2], mod[:, 3], mod[:, 4], mod[:, 5])
    ga = (2 * (ga >= 0) - 1) * jnp.maximum(jnp.abs(ga), 0.25)
    gb = (2 * (gb >= 0) - 1) * jnp.maximum(jnp.abs(gb), 0.25)
    h = _layernorm(x, axis=-1) * (1 + ca) + sa
    x = x + ga * _L1_attn_ref(h, L1_attn_Wq, L1_attn_Wk, L1_attn_Wv, L1_attn_Wo)
    h = _layernorm(x, axis=-1) * (1 + cb) + sb
    x = x + gb * _L1_ffn_ref(h, L1_ffn_W, L1_ffn_b, L1_ffn_lora_down, L1_ffn_lora_up, L1_ffn_down_aux, L1_ffn_up_aux)
    return x

_drawn_inputs = setup_inputs


def setup_inputs(seed=0):
    import zlib

    import numpy as np

    out = dict(_drawn_inputs(seed))
    spreads = {'L0_attn_b_proj': (0.0, 0.305)}
    factors = {'L0_ffn_W_r': 8.0,
     'L0_ffn_W_k': 3.019,
     'L0_ffn_W_v': 2.765,
     'L0_ffn_mu_r': 8.0,
     'L0_ffn_mu_k': 5.006,
     'L1_attn_Wq': 8.0,
     'L1_attn_Wk': 8.0,
     'L1_attn_Wv': 8.0,
     'L1_attn_Wo': 8.0,
     'L1_ffn_b': 200.0,
     'L1_ffn_lora_down': 8.0,
     'L1_ffn_lora_up': 8.0,
     'L1_ffn_down_aux': 8.0,
     'L1_ffn_up_aux': 8.0,
     'L1_ffn_W': 8.0}
    for name, (base, spread) in spreads.items():
        noise = np.random.default_rng([zlib.crc32(name.encode()), seed]).standard_normal(out[name].shape)
        drawn = base * np.exp(spread * noise) if base else spread * noise
        out[name] = jnp.asarray(drawn.astype(out[name].dtype))
    for name, factor in factors.items():
        out[name] = (out[name] * factor).astype(out[name].dtype)
    return out
```

```python
import numpy as np

import concourse.bass as bass
from concourse import mybir
from contextlib import ExitStack

B, T, D = 8, 1024, 256
H, DH = 16, 16
P = 128
NT = T // P
FC = D // P
GH = 4
NG = H // GH
HPT = P // DH
BANK = 512
HALF = 2 * BANK
LAYERS = 2
EPS = 1e-5
SCALE = 0.25
NEG = -1e30

Q_PARTS = (0, 0, 1, 1)
K_PARTS = (0, 1, 0, 1)
ROW_ALIBI = len(Q_PARTS) * DH
N_ALIBI = 3
ROW_MAX = ROW_ALIBI + N_ALIBI
N_MAX = 2
MAX_UNIT = 64.0
K_USED = ROW_MAX + N_MAX


def score_turns():
    turns = []
    for kt in range(NT):
        n = 1 if kt < NT // 2 else (2 if kt < 6 else 4)
        turns += [(kt, tuple(range(h, h + n))) for h in range(0, GH, n)]
    return turns


def max_steps():
    steps = []
    for g in range(NG):
        own = [("max", g, h, qt, half) for h in range(GH) for qt in range(NT)
               for half in range(1 if qt < NT // 2 else 2)]
        if g:
            own.insert(3, ("turn", g - 1))
        steps += own
    return steps + [("turn", NG - 1)]


SCORE_TURNS = score_turns()
MAX_STEPS = max_steps()
STEPS_G = len([s for s in MAX_STEPS if s[0] == "max"]) // NG
LEAD = STEPS_G + 13
NORM_AT = STEPS_G * 3 // 4



def main_items():
    turns = [(g, i) for g in range(NG) for i in range(len(SCORE_TURNS))]
    behind = {}
    for n, (g, i) in enumerate(turns):
        kt = SCORE_TURNS[i][0]
        if i + 1 == len(SCORE_TURNS) or SCORE_TURNS[i + 1][0] != kt:
            for j, bank in enumerate(range(kt * P // BANK, T // BANK)):
                behind.setdefault(n + 2 + j, []).append(("context", g, kt, bank))
    items = []
    for n in range(len(turns) + 4):
        if n < len(turns):
            items.append(("score", *turns[n]))
        items += behind.get(n, [])
    return items


def item_columns(item):
    if item[0] == "score":
        kt, heads = SCORE_TURNS[item[2]]
        return len(heads) * (T - kt * P)
    return 4 * ((item[3] + 1) * BANK - max(item[2] * P, item[3] * BANK))


def step_end():
    ends, at = [], 0
    for step in MAX_STEPS:
        wide = step[0] == "max" and step[3] >= NT // 2 and step[4] == 0
        at += 256 if step[0] == "turn" else (BANK if wide else (step[3] % 4 + 1) * P) + 80
        ends.append(at)
    return ends


MAIN_ITEMS = main_items()
STEP_END = step_end()
PACE = 1.06 * STEP_END[-1] / sum(item_columns(m) for m in MAIN_ITEMS)

T_ROPE = 2 * FC
ATTN_TURNS = [2 + 4 + 2 + NG * len(SCORE_TURNS) + 2, 2 + 4 + T_ROPE + 2 + NG * len(SCORE_TURNS) + 2]
FFN_TURNS = [2 + 2 + 2 + 2, 2 + 2]
TURNS = sum(ATTN_TURNS) + sum(FFN_TURNS)
assert TURNS % 2 == 0
V_CHAIN = 135
G_CHAIN = 3


def adaln_program(nc, x, c0, c1, wmod0, wmod1, wqkv, wout, bias, wffn, mu, lora, wbase, rope, rows_c, out):
    f32, f16, bf16, i32 = mybir.dt.float32, mybir.dt.float16, mybir.dt.bfloat16, mybir.dt.int32
    ALU = mybir.AluOpType
    ACT = mybir.ActivationFunctionType
    AX = mybir.AxisListType.X
    down_t, down_aux, up_t, up_aux_t = lora
    perm, cos, sin = rope
    alibi_rows, zero_rows, one_rows, unit_rows = rows_c

    parts_dram = nc.dram_tensor("parts_dram", (2, FC, 2, P, T), f16, kind="Internal").ap()
    gate_dram = nc.dram_tensor("gate_dram", (B, 2 * LAYERS, D), f32, kind="Internal").ap()

    ctx = ExitStack()
    with ctx:
        def sb(name, shape, dt=f32):
            return ctx.enter_context(nc.sbuf_tensor(name, shape, dt))

        def sem(name):
            return ctx.enter_context(nc.semaphore(name))

        x_in = sb("x_in", [P, NT, D])
        x_res = sb("x_res", [P, NT, D])
        hT = sb("hT", [P, FC, T + 1])
        stack_q = sb("stack_q", [P, H, T], f16)
        stack_k = sb("stack_k", [P, H, T], f16)
        v_ones = sb("v_ones", [P, NT, H, 2 * DH])
        probs = sb("probs", [P, 2, GH, T])
        ctx_u = sb("ctx_u", [P, T])
        ctx_b = sb("ctx_b", [P, T])
        ctxT = sb("ctxT", [P, NG, T])
        mask = sb("mask", [P, BANK])
        mx = sb("mx", [P, 2, GH * NT, 2])
        mxc = sb("mxc", [P, 2, GH * NT])
        m_hi = sb("m_hi", [GH * NT, 2, P], f16)
        m_lo = sb("m_lo", [GH * NT, 2, P], f16)
        w_qkv = sb("w_qkv", [P, 3, FC, D])
        w_out = sb("w_out", [P, NG, D])
        w_out_g = sb("w_out_g", [P, NG, D])
        w_ffn = sb("w_ffn", [P, 3, FC, D])
        w_lin = sb("w_lin", [P, FC, D])
        w_last_g = sb("w_last_g", [P, FC, D])
        gates = sb("gates", [P, 2 * LAYERS, D])
        bias_bc = sb("bias_bc", [P, 2, D])
        bias_g = sb("bias_g", [P, D])
        modT = sb("modT", [P, 16, B])
        modc = sb("modc", [P, 16])
        mu_c = sb("mu_c", [P, 2, FC])
        ident = sb("ident", [P, P])
        perm_sb = sb("perm_sb", [P, P])
        cos_sb = sb("cos_sb", [P, T])
        sin_sb = sb("sin_sb", [P, T])
        stats = sb("stats", [P, NT, 6])
        mv = sb("mv", [P, NT, 2])
        ve = sb("ve", [P, NT])
        rstd = sb("rstd", [P, NT])
        tmp = sb("tmp", [P, NT])
        nmr = sb("nmr", [P, NT])
        region = probs[:].rearrange("p a h t -> p (a h t)")
        qk32 = region[:, 0:4 * T].rearrange("p (w f t) -> p w f t", w=2, f=FC)
        rope_sin = region[:, 4 * T:6 * T].rearrange("p (a t) -> p a t", a=2)
        rope_cos = region[:, 6 * T:8 * T].rearrange("p (a t) -> p a t", a=2)
        mix_r = region[:, 0:2 * T].rearrange("p (f t) -> p f t", f=FC)
        mix_k = region[:, 2 * T:4 * T].rearrange("p (f t) -> p f t", f=FC)
        k_act = region[:, 4 * T:6 * T].rearrange("p (f t) -> p f t", f=FC)
        r_gate = region[:, 6 * T:8 * T].rearrange("p (t n) -> p t n", t=NT)
        v_prod = ctx_u[:, :]
        xn = ctxT[:, 0:2, :].rearrange("p g t -> p (g t)").rearrange("p (t n) -> p t n", t=NT)
        parts = ctxT[:, :, :].rearrange("p g t -> p (g t)").bitcast(f16)\
            .rearrange("p (w f s t) -> p w f s t", w=2, f=FC, s=2)
        wmod_sb = region[:, 0:6 * T].rearrange("p (l c n) -> p l c n", l=2, c=FC)
        region2 = hT[:].rearrange("p f t -> p (f t)")
        silu_in = stats[:].rearrange("p a b -> p (a b)")[:, 0:32].rearrange("p (l c b) -> p l c b", l=2, c=FC)
        silu_e = w_last_g[:, 0, 0:32].rearrange("p (l c b) -> p l c b", l=2, c=FC)
        silu_o = mx[:].rearrange("p a b c -> p (a b c)")[:, 0:32].rearrange("p (l c b) -> p l c b", l=2, c=FC)
        gate_raw = x_res[0:B, 0:4, :].rearrange("b t n -> b (t n)")
        gate_neg = x_res[0:B, 4:8, :].rearrange("b t n -> b (t n)")
        gate_abs = x_in[0:B, 0:4, :].rearrange("b t n -> b (t n)")
        gate_sgn = x_in[0:B, 4:8, :].rearrange("b t n -> b (t n)")
        lora_a = region2[0:100, 0:4]
        lora_b = region2[0:100, 8:8 + D]
        lora_c = region2[0:4, 272:322]
        lora_d = region2[0:50, 328:328 + D]
        lora_1 = region2[0:4, 592:592 + D]
        lora_2 = region2[0:50, 856:856 + D]

        big = ctx.enter_context(nc.psum_tensor("big", [P, 2, HALF], f32))
        ctx_ps = ctx.enter_context(nc.psum_tensor("ctx_ps", [P, HALF], f32))
        small = ctx.enter_context(nc.psum_tensor("small", [P, 2, BANK], f32))

        consts_in = sem("consts_in")
        consts_set = sem("consts_set")
        silu_exp = sem("silu_exp")
        stacks_clear = sem("stacks_clear")
        pro_mm = sem("pro_mm")
        pro_v = sem("pro_v")
        gates_out = sem("gates_out")
        x_loaded = sem("x_loaded")
        gates_loaded = sem("gates_loaded")
        w_loaded = sem("w_loaded")
        wout_loaded = sem("wout_loaded")
        rows_loaded = sem("rows_loaded")
        filled = sem("filled")
        freed = [sem("freed_0"), sem("freed_1")]
        s_filled = sem("s_filled")
        s_freed = sem("s_freed")
        xn_ready = sem("xn_ready")
        modc_ready = sem("modc_ready")
        parts_ready = sem("parts_ready")
        parts_saved = [sem("parts_saved_0"), sem("parts_saved_1")]
        stacked = [sem("stacked_0"), sem("stacked_1")]
        rope_ready = sem("rope_ready")
        rope_cos_ready = sem("rope_cos_ready")
        max_ready = sem("max_ready")
        mrow_loaded = [sem("mrow_loaded_0"), sem("mrow_loaded_1")]
        masked = sem("masked")
        pv_done = sem("pv_done")
        ctx_saved = sem("ctx_saved")
        ctx_ready = sem("ctx_ready")
        w_scaled = sem("w_scaled")
        biased = sem("biased")
        mix_ready = sem("mix_ready")
        act_ready = sem("act_ready")
        stored = sem("stored")
        v_chain = sem("v_chain")
        g_chain = sem("g_chain")
        waits_taken = sem("waits_taken")

        first_turn = {}
        n = 0
        for layer in range(LAYERS):
            for name, size in [("norm", 2)] + ([("qk", 4)] if layer == 0 else [("qk", 4), ("rope", T_ROPE)]) + \
                    [("v", 2), ("score", NG * len(SCORE_TURNS)), ("proj", 2), ("norm2", 2)] + \
                    ([("r", 2), ("k", 2)] if layer == 0 else []) + [("y", 2)]:
                first_turn[name, layer] = n
                n += size
        assert n == TURNS

        def wait_filled(eng, it, turn):
            eng.wait_ge(filled, it * TURNS + turn + 1)

        def wait_emptied(eng, it, turn):
            eng.wait_ge(freed[turn % 2], it * (TURNS // 2) + turn // 2 + 2)

        def wait_half(eng, it, turn):
            eng.wait_ge(freed[turn % 2], it * (TURNS // 2) + turn // 2 + 1)

        def settle(eng):
            eng.sem_inc(waits_taken, 1)

        n_consts = 20
        block = ctx.enter_context(nc.Block())

        @block.sync
        def _(sp):
            def load(dst, src):
                sp.dma_start(dst, src).then_inc(consts_in, 16)

            for l, (c, w) in enumerate(((c0, wmod0), (c1, wmod1))):
                load(silu_in[:, l], c.rearrange("(c p) b -> p c b", p=P))
                load(wmod_sb[:, l], w.rearrange("(c p) n -> p c n", p=P))
            for w in range(3):
                load(w_ffn[:, w], wffn[w].rearrange("(c p) n -> p c n", p=P))
            load(w_lin[:], wbase.rearrange("(c p) n -> p c n", p=P))
            load(lora_a, down_t)
            load(lora_b, down_aux)
            load(lora_c, up_t)
            load(lora_d, up_aux_t)
            load(mu_c[:].rearrange("p w c -> p (w c)"), mu)
            load(perm_sb[:], perm)
            load(cos_sb[:], cos)
            load(sin_sb[:], sin)
            for w in range(2):
                load(bias_bc[:, w], bias[w:w + 1, :].broadcast_to([P, D]))
            sp.wait_ge(stacks_clear, 2)
            load(stack_q[ROW_ALIBI:ROW_MAX], one_rows)
            load(stack_k[ROW_MAX:K_USED], unit_rows)
            sp.wait_ge(pro_v, 5)
            sp.dma_start(gate_dram.rearrange("b g n -> b (g n)"), gate_raw).then_inc(gates_out, 16)
            sp.wait_ge(gates_out, 16)
            sp.dma_start(x_in[:], x[0].rearrange("(t p) n -> p t n", p=P)).then_inc(x_loaded, 16)
            with sp.Fori(0, B) as it:
                for n in range(2):
                    wait_emptied(sp, it - 1, first_turn["y", 1] + n)
                sp.dma_start(gates[:].rearrange("p g n -> p (g n)"),
                             gate_dram[bass.ds(it, 1)].rearrange("o g n -> o (g n)").broadcast_to([P, 4 * D]))\
                    .then_inc(gates_loaded, 16)
                for layer in range(LAYERS):
                    call = it * LAYERS + layer
                    if layer:
                        for n in range(2):
                            wait_emptied(sp, it, first_turn["proj", 0] + n)
                    sp.dma_start(w_qkv[:], wqkv[layer].rearrange("w (c p) n -> p w c n", p=P)).then_inc(w_loaded, 16)
                    sp.dma_start(w_out[:], wout[layer].rearrange("(g p) n -> p g n", p=P)).then_inc(wout_loaded, 16)
                    sp.dma_start(stack_k[ROW_ALIBI:ROW_MAX], alibi_rows if layer == 0 else zero_rows)\
                        .then_inc(rows_loaded, 16)
                    sp.dma_start(stack_q[ROW_MAX:K_USED], zero_rows[0:N_MAX]).then_inc(rows_loaded, 16)
                    for ft in range(FC):
                        for w in range(2):
                            sp.wait_ge(parts_ready, call * 4 + 2 * ft + w + 1)
                            sp.dma_start(parts_dram[w, ft].rearrange("s p t -> p s t"), parts[:, w, ft])\
                                .then_inc(parts_saved[ft], 16)
                        sp.wait_ge(parts_saved[ft], call * 32 + 32)
                        for w, (stack, order) in enumerate(((stack_q, Q_PARTS), (stack_k, K_PARTS))):
                            for r, s in enumerate(order):
                                sp.dma_start(stack[r * DH:(r + 1) * DH, ft * HPT:(ft + 1) * HPT, :],
                                             parts_dram[w, ft, s].rearrange("(h d) t -> d h t", d=DH))\
                                    .then_inc(stacked[ft], 16)
                    for g in range(NG):
                        sp.wait_ge(s_freed, call * len(MAX_STEPS) + MAX_STEPS.index(("turn", g)) + 1 + 2)
                        for r, m in enumerate((m_hi, m_lo)):
                            sp.dma_start(stack_q[ROW_MAX + r:ROW_MAX + r + 1, g * GH:(g + 1) * GH, :]
                                         .rearrange("r h (q t) -> r (h q) t", t=P), m[:, g % 2, :])\
                                .then_inc(mrow_loaded[g % 2], 16)
                    if layer == 0:
                        for n in range(2):
                            wait_emptied(sp, it, first_turn["proj", 0] + n)
                        sp.dma_start(x_in[:], x[bass.ds((it + 1) % B, 1)].rearrange("o (t p) n -> p (o t) n", p=P))\
                            .then_inc(x_loaded, 16)
                for n in range(2):
                    wait_emptied(sp, it, first_turn["y", 1] + n)
                sp.dma_start(out[bass.ds(it, 1)].rearrange("o (t p) n -> p (o t) n", p=P), x_res[:]).then_inc(stored, 16)
            sp.wait_ge(stored, 16 * (B + 1))
            sp.wait_ge(x_loaded, 16 * (B + 1))

        @block.gpsimd
        def _(pool):
            g = nc.gpsimd
            g.memset(ident[:], 0.0).then_inc(g_chain, 1)
            g.memset(mask[:], 0.0).then_inc(g_chain, 1)
            g.memset(v_ones[:], 1.0).then_inc(consts_set, 1)
            pool.wait_ge(g_chain, 2)
            g.affine_select(out=ident[:], in_=ident[:], compare_op=ALU.not_equal, fill=1.0, base=0,
                            pattern=[[-1, P]], channel_multiplier=1).then_inc(consts_set, 1)
            g.affine_select(out=mask[:, BANK - P:], in_=mask[:, BANK - P:], compare_op=ALU.is_ge, fill=NEG, base=0,
                            pattern=[[-1, P]], channel_multiplier=1).then_inc(consts_set, 1)
            pool.wait_ge(consts_in, 16 * n_consts)
            with pool.Fori(0, B) as it:
                chain = [0]

                def link(ins):
                    chain[0] += 1
                    ins.then_inc(g_chain, 1)
                    pool.wait_ge(g_chain, it * G_CHAIN + chain[0] + 2)

                pool.wait_ge(gates_loaded, it * 16 + 16)
                for layer in range(LAYERS):
                    call = it * LAYERS + layer
                    pool.wait_ge(wout_loaded, call * 16 + 16)
                    g.tensor_tensor(w_out_g[:], w_out[:], gates[:, 2 * layer:2 * layer + 1, :].broadcast_to([P, NG, D]),
                                    ALU.mult).then_inc(w_scaled, 1)
                    if layer == 0:
                        link(g.tensor_tensor(bias_g[:], gates[:, 0, :], bias_bc[:, 0, :], ALU.mult))
                        pool.wait_ge(xn_ready, it * 4 + 1)
                        g.tensor_tensor(x_in[:], x_in[:], bias_g[:].rearrange("p (o n) -> p o n", o=1)
                                        .broadcast_to([P, NT, D]), ALU.add).then_inc(biased, 1)
                    else:
                        for ft in range(FC):
                            for w in range(2):
                                turn = first_turn["qk", 1] + 2 * ft + w
                                wait_emptied(pool, it, turn)
                                if ft * 2 + w >= 2:
                                    pool.wait_ge(parts_ready, call * 4 + 2 * ft + w - 1)
                                g.tensor_tensor(rope_cos[:, w], qk32[:, w, ft], cos_sb[:], ALU.mult)\
                                    .then_inc(rope_cos_ready, 1)
                    for gr in range(NG):
                        for kt in range(NT):
                            last = max(i for i, (k, _) in enumerate(SCORE_TURNS) if k == kt)
                            turn = first_turn["score", layer] + gr * len(SCORE_TURNS) + last
                            wait_emptied(pool, it, turn)
                            wait_emptied(pool, it, turn - 1)
                            settle(pool)
                            diag = probs[:, kt % 2, :, kt * P:(kt + 1) * P]
                            g.affine_select(out=diag, in_=diag, compare_op=ALU.is_ge, fill=0.0, base=0,
                                            pattern=[[0, GH], [1, P]], channel_multiplier=-1).then_inc(masked, 1)
                    if layer == 0:
                        link(g.tensor_scalar(bias_g[:], gates[:, 1, :], 0.5, None, ALU.mult))
                        g.tensor_tensor(w_last_g[:], w_ffn[:, 2], bias_g[:].rearrange("p (o n) -> p o n", o=1)
                                        .broadcast_to([P, FC, D]), ALU.mult).then_inc(w_scaled, 1)
                    else:
                        link(g.tensor_tensor(bias_g[:], gates[:, 3, :], bias_bc[:, 1, :], ALU.mult))
                        g.tensor_tensor(w_last_g[:], w_lin[:], gates[:, 3:4, :].broadcast_to([P, FC, D]),
                                        ALU.mult).then_inc(w_scaled, 1)
                        pool.wait_ge(xn_ready, it * 4 + 4)
                        g.tensor_tensor(x_res[:], x_res[:], bias_g[:].rearrange("p (o n) -> p o n", o=1)
                                        .broadcast_to([P, NT, D]), ALU.add).then_inc(biased, 1)

        @block.scalar
        def _(act):
            s = nc.scalar
            act.wait_ge(consts_in, 16 * n_consts)
            s.activation(silu_e, silu_in, ACT.Exp, scale=-1.0).then_inc(silu_exp, 1)
            with act.Fori(0, B) as it:
                for layer in range(LAYERS):
                    call = it * LAYERS + layer
                    groups = call * NG

                    def norm_turns(which):
                        if layer == 0 and which == 0:
                            act.wait_ge(modc_ready, it + 1)
                        for fc in range(FC):
                            turn = first_turn["norm" if which == 0 else "norm2", layer] + fc
                            col = layer * 8 + which * 2 + fc
                            wait_filled(act, it, turn)
                            s.activation(hT[:, fc, 1:], big[:, turn % 2, :], ACT.Identity,
                                         scale=modc[:, col + 4:col + 5], bias=modc[:, col:col + 1])\
                                .then_inc(freed[turn % 2], 1)

                    norm_turns(0)
                    for ft in range(FC):
                        for w in range(2):
                            turn = first_turn["qk", layer] + 2 * ft + w
                            wait_filled(act, it, turn)
                            s.activation(qk32[:, w, ft], big[:, turn % 2, :], ACT.Copy, scale=SCALE if w == 0 else 1.0)\
                                .then_inc(freed[turn % 2], 1)
                    for n in range(2):
                        turn = first_turn["v", layer] + n
                        wait_filled(act, it, turn)
                        s.activation(v_ones[:, n * 4:(n + 1) * 4, :, 0:DH],
                                     big[:, turn % 2, :].rearrange("p (t h d) -> p t h d", t=4, h=H), ACT.Copy)\
                            .then_inc(freed[turn % 2], 1)

                    def save_context(g):
                        act.wait_ge(pv_done, (groups + g) * NT + NT + 2)
                        act.wait_ge(ctx_ready, groups + g + 1)
                        s.activation(ctx_u[:], ctx_ps[:], ACT.Copy).then_inc(ctx_saved, 1)

                    for g in range(NG):
                        for i, (kt, heads) in enumerate(SCORE_TURNS):
                            turn = first_turn["score", layer] + g * len(SCORE_TURNS) + i
                            wait_filled(act, it, turn)
                            if heads[0] == 0:
                                act.wait_ge(pv_done, (groups + g) * NT + kt + 1)
                            q0 = kt * P
                            if len(heads) == 1:
                                dst = probs[:, kt % 2, heads[0], q0:]
                                src = big[:, turn % 2, q0:]
                            else:
                                n = T - q0
                                dst = probs[:, kt % 2, heads[0]:heads[-1] + 1, q0:]
                                src = big[:, turn % 2, :].rearrange("p (h q) -> p h q", h=len(heads))[:, :, 0:n]
                            s.activation(dst, src, ACT.Exp).then_inc(freed[turn % 2], 1)
                            if g and i == GH:
                                save_context(g - 1)
                    save_context(NG - 1)
                    norm_turns(1)
                    if layer == 0:
                        for n in range(2):
                            turn = first_turn["r", 0] + n
                            wait_filled(act, it, turn)
                            s.activation(r_gate[:, n * 4:(n + 1) * 4, :],
                                         big[:, turn % 2, :].rearrange("p (t n) -> p t n", t=4), ACT.Tanh, scale=0.5)\
                                .then_inc(freed[turn % 2], 1)
                        for ft in range(FC):
                            turn = first_turn["k", 0] + ft
                            wait_filled(act, it, turn)
                            s.activation(k_act[:, ft], big[:, turn % 2, :], ACT.Relu).then_inc(freed[turn % 2], 1)

        @block.vector
        def _(dve):
            v = nc.vector
            for stack in (stack_q, stack_k):
                v.memset(stack[P // 2:], 0.0).then_inc(stacks_clear, 1)
            for half in freed:
                dve.sem_inc(half, 1)
            dve.sem_inc(s_freed, 2)
            dve.sem_inc(pv_done, 2)
            dve.sem_inc(ctx_ready, 1)
            dve.sem_inc(stored, 16)
            dve.wait_ge(consts_in, 16 * n_consts)
            dve.wait_ge(silu_exp, 1)
            v.tensor_scalar_add(silu_e, silu_e, 1.0).then_inc(pro_v, 1)
            dve.wait_ge(pro_v, 1)
            v.reciprocal(silu_e, silu_e).then_inc(pro_v, 1)
            dve.wait_ge(pro_v, 2)
            v.tensor_tensor(silu_o, silu_in, silu_e, ALU.mult).then_inc(pro_v, 1)
            dve.wait_ge(pro_mm, 1)
            v.tensor_copy(gate_raw, ctx_ps[0:B, :]).then_inc(v_chain, 1)
            dve.wait_ge(v_chain, 1)
            v.tensor_scalar(gate_neg, gate_raw, -1.0, None, ALU.mult).then_inc(v_chain, 1)
            v.tensor_scalar(gate_sgn, gate_raw, 0.0, 2.0, ALU.is_ge, ALU.mult).then_inc(v_chain, 1)
            dve.wait_ge(v_chain, 3)
            v.tensor_tensor(gate_abs, gate_raw, gate_neg, ALU.max).then_inc(v_chain, 1)
            dve.wait_ge(v_chain, 4)
            v.tensor_scalar(gate_sgn, gate_sgn, -1.0, None, ALU.add).then_inc(v_chain, 1)
            v.tensor_scalar(gate_abs, gate_abs, 0.25, None, ALU.max).then_inc(v_chain, 1)
            dve.wait_ge(v_chain, 6)
            v.tensor_tensor(gate_raw, gate_sgn, gate_abs, ALU.mult).then_inc(v_chain, 1)
            dve.wait_ge(pro_mm, 2)
            ps_mod = small[:, 0, 0:16 * B].rearrange("p (k b) -> p k b", b=B)
            for l in range(LAYERS):
                v.tensor_copy(modT[:, 8 * l:8 * l + 4, :], ps_mod[:, 8 * l:8 * l + 4, :]).then_inc(v_chain, 1)
                v.tensor_scalar_add(modT[:, 8 * l + 4:8 * l + 8, :], ps_mod[:, 8 * l + 4:8 * l + 8, :], 1.0)\
                    .then_inc(v_chain, 1)
            dve.wait_ge(pro_mm, 3)
            v.tensor_copy(lora_1, small[0:4, 1, 0:D]).then_inc(pro_v, 1)
            dve.wait_ge(v_chain, 11)
            v.memset(mx[:], 3.0 * NEG).then_inc(pro_v, 1)
            dve.wait_ge(pro_mm, 4)
            v.tensor_copy(lora_2, small[0:50, 1, D:2 * D]).then_inc(pro_v, 1)
            dve.wait_ge(pro_mm, 5)
            v.tensor_tensor(w_lin[:], w_lin[:], small[:, 0, :].rearrange("p (c n) -> p c n", c=FC), ALU.add)\
                .then_inc(v_chain, 1)
            dve.wait_ge(v_chain, 12)
            v.memset(hT[:, :, 0:1], 0.0).then_inc(pro_v, 1)
            CH0 = 12

            with dve.Fori(0, B) as it:
                chain = [0]

                def link(ins):
                    chain[0] += 1
                    ins.then_inc(v_chain, 1)
                    dve.wait_ge(v_chain, it * V_CHAIN + chain[0] + CH0)

                def layernorm(src, which):
                    for t in range(NT - 1):
                        v.bn_stats(stats[:, t, :], src[:, t, :])
                    link(v.bn_stats(stats[:, NT - 1, :], src[:, NT - 1, :]))
                    settle(dve)
                    for t in range(NT - 1):
                        v.bn_aggr(mv[:, t, :], stats[:, t, :])
                    link(v.bn_aggr(mv[:, NT - 1, :], stats[:, NT - 1, :]))
                    link(v.tensor_scalar_add(ve[:], mv[:, :, 1], EPS))
                    link(v.tensor_scalar(tmp[:].bitcast(i32), ve[:].bitcast(i32), 1, None, ALU.logical_shift_right))
                    link(v.tensor_scalar(rstd[:].bitcast(i32), tmp[:].bitcast(i32), -1.0, float(0x5F3759DF),
                                         ALU.mult, ALU.add))
                    for _ in range(4):
                        link(v.tensor_tensor(tmp[:], rstd[:], rstd[:], ALU.mult))
                        link(v.tensor_tensor(tmp[:], tmp[:], ve[:], ALU.mult))
                        link(v.tensor_scalar(tmp[:], tmp[:], -0.5, 1.5, ALU.mult, ALU.add))
                        link(v.tensor_tensor(rstd[:], rstd[:], tmp[:], ALU.mult))
                    link(v.scalar_tensor_tensor(out=nmr[:], in0=mv[:, :, 0], scalar=-1.0, in1=rstd[:],
                                                op0=ALU.mult, op1=ALU.mult))
                    for t in range(NT):
                        last = v.tensor_scalar(xn[:, t, :], src[:, t, :], rstd[:, t:t + 1], nmr[:, t:t + 1],
                                               ALU.mult, ALU.add)
                    last.then_inc(xn_ready, 1)

                v.tensor_copy(modc[:], modT[:, :, bass.ds(it, 1)].rearrange("p k o -> p (k o)"))\
                    .then_inc(modc_ready, 1)
                for layer in range(LAYERS):
                    call = it * LAYERS + layer
                    groups = call * NG
                    src = x_in if layer == 0 else x_res
                    if layer == 0:
                        dve.wait_ge(x_loaded, it * 16 + 16)
                    layernorm(src, 0)

                    for ft in range(FC):
                        for w in range(2):
                            turn = first_turn["qk", layer] + 2 * ft + w
                            wait_emptied(dve, it, turn)
                            own = qk32[:, w, ft]
                            if layer == 1:
                                turn = first_turn["rope", 1] + 2 * ft + w
                                wait_filled(dve, it, turn)
                                v.tensor_tensor(rope_sin[:, w], big[:, turn % 2, :], sin_sb[:], ALU.mult)\
                                    .then_inc(freed[turn % 2], 1)
                                wait_emptied(dve, it, turn)
                                dve.wait_ge(rope_cos_ready, it * 4 + 2 * ft + w + 1)
                                link(v.tensor_tensor(own, rope_cos[:, w], rope_sin[:, w], ALU.add))
                            link(v.tensor_copy(parts[:, w, ft, 0], own))
                            v.tensor_tensor(parts[:, w, ft, 1], own, parts[:, w, ft, 0], ALU.subtract)\
                                .then_inc(parts_ready, 1)

                    def normalise(g):
                        dve.wait_ge(ctx_saved, groups + g + 1)
                        link(v.transpose(ctx_b[:], ctx_u[:]))
                        blk = ctx_b[:].rearrange("p (c r) -> p c r", r=32)
                        link(v.reciprocal(blk[:, :, DH:DH + 1], blk[:, :, DH:DH + 1]))
                        link(v.tensor_tensor(blk[:, :, 0:DH], blk[:, :, 0:DH],
                                             blk[:, :, DH:DH + 1].broadcast_to([P, T // 32, DH]), ALU.mult))
                        v.transpose(ctxT[:, g, :], ctx_b[:]).then_inc(ctx_ready, 1)

                    done = 0
                    for n, step in enumerate(MAX_STEPS):
                        dve.wait_ge(s_filled, call * len(MAX_STEPS) + n + 1)
                        if step[0] == "max":
                            _, g, h, qt, half = step
                            to = mx[:, g % 2, h * NT + qt, half:half + 1]
                            if qt >= NT // 2 and half == 0:
                                ins = v.reduce_max(to, small[:, n % 2, :], AX)
                            else:
                                width = (qt % 4 + 1) * P
                                settle(dve)
                                ins = v.tensor_tensor_reduce(
                                    out=small[:, n % 2, 0:width], in0=small[:, n % 2, 0:width], in1=mask[:, BANK - width:],
                                    scale=1.0, scalar=3.0 * NEG, op0=ALU.add, op1=ALU.max, accum_out=to)
                            ins.then_inc(s_freed, 1)
                            done += 1
                            if done % STEPS_G == 0:
                                dve.wait_ge(s_freed, call * len(MAX_STEPS) + n + 1 + 2)
                                v.tensor_tensor(mxc[:, g % 2, :], mx[:, g % 2, :, 0], mx[:, g % 2, :, 1], ALU.max)\
                                    .then_inc(max_ready, 1)
                        else:
                            g = step[1]
                            turned = small[0:GH * NT, n % 2, 0:P]
                            link(v.tensor_scalar(m_hi[:, g % 2, :], turned, -1.0 / MAX_UNIT, None, ALU.mult))
                            v.scalar_tensor_tensor(out=m_lo[:, g % 2, :], in0=turned, scalar=-1.0 / MAX_UNIT,
                                                   in1=m_hi[:, g % 2, :], op0=ALU.mult, op1=ALU.subtract)\
                                .then_inc(s_freed, 1)
                        g = done // STEPS_G - 2
                        if step[0] == "max" and 0 <= g < NG - 2 and done % STEPS_G == NORM_AT:
                            normalise(g)
                    for g in range(NG - 2, NG):
                        normalise(g)

                    if layer == 0:
                        dve.wait_ge(biased, it * 2 + 1)
                        dve.wait_ge(stored, it * 16 + 16)
                    for n in range(2):
                        turn = first_turn["proj", layer] + n
                        wait_filled(dve, it, turn)
                        v.tensor_tensor(x_res[:, n * 4:(n + 1) * 4, :], src[:, n * 4:(n + 1) * 4, :],
                                        big[:, turn % 2, :].rearrange("p (t n) -> p t n", t=4), ALU.add)\
                            .then_inc(freed[turn % 2], 1)
                        wait_emptied(dve, it, turn)
                    layernorm(x_res, 1)

                    if layer == 0:
                        wait_emptied(dve, it, first_turn["norm2", 0])
                        wait_emptied(dve, it, first_turn["norm2", 0] + 1)
                        link(v.tensor_tensor(k_act, hT[:, :, 1:], hT[:, :, 0:T], ALU.subtract))
                        for w, mix in enumerate((mix_r, mix_k)):
                            for fc in range(FC):
                                v.scalar_tensor_tensor(out=mix[:, fc], in0=k_act[:, fc], scalar=mu_c[:, w, fc:fc + 1],
                                                       in1=hT[:, fc, 0:T], op0=ALU.mult, op1=ALU.add)\
                                    .then_inc(mix_ready, 1)
                        for ft in range(FC):
                            wait_emptied(dve, it, first_turn["k", 0] + ft)
                            v.tensor_tensor(k_act[:, ft], k_act[:, ft], k_act[:, ft], ALU.mult).then_inc(act_ready, 1)
                    else:
                        dve.wait_ge(biased, it * 2 + 2)
                    for n in range(2):
                        turn = first_turn["y", layer] + n
                        wait_filled(dve, it, turn)
                        add = big[:, turn % 2, :].rearrange("p (t n) -> p t n", t=4)
                        own = x_res[:, n * 4:(n + 1) * 4, :]
                        if layer == 0:
                            prod = v_prod.rearrange("p (t n) -> p t n", t=4)
                            v.scalar_tensor_tensor(out=prod, in0=r_gate[:, n * 4:(n + 1) * 4, :], scalar=1.0, in1=add,
                                                   op0=ALU.add, op1=ALU.mult).then_inc(freed[turn % 2], 1)
                            wait_emptied(dve, it, turn)
                            link(v.tensor_tensor(own, own, prod, ALU.add))
                        else:
                            v.tensor_tensor(own, own, add, ALU.add).then_inc(freed[turn % 2], 1)
                            wait_emptied(dve, it, turn)
                assert chain[0] == V_CHAIN, chain[0]

        @block.tensor
        def _(pe):
            te = nc.tensor
            pe.wait_ge(consts_in, 16 * n_consts)
            pe.wait_ge(consts_set, 3)
            pe.wait_ge(pro_v, 3)
            for gi in range(2 * LAYERS):
                l, part = gi // 2, (2, 5)[gi % 2]
                for c in range(FC):
                    last = te.matmul(ctx_ps[0:B, gi * D:(gi + 1) * D], silu_o[:, l, c, :],
                                     wmod_sb[:, l, c, part * D:(part + 1) * D], start=(c == 0), stop=(c == FC - 1))
            last.then_inc(pro_mm, 1)
            for l in range(LAYERS):
                for k, part in enumerate((0, 3, 1, 4)):
                    for fc in range(FC):
                        col = (8 * l + 2 * k + fc) * B
                        for c in range(FC):
                            last = te.matmul(small[:, 0, col:col + B],
                                             wmod_sb[:, l, c, part * D + fc * P:part * D + (fc + 1) * P],
                                             silu_o[:, l, c, :], start=(c == 0), stop=(c == FC - 1))
            last.then_inc(pro_mm, 1)
            te.matmul(small[0:4, 1, 0:D], lora_a, lora_b, start=True, stop=True).then_inc(pro_mm, 1)
            pe.wait_ge(pro_v, 4)
            te.matmul(small[0:50, 1, D:2 * D], lora_c, lora_1, start=True, stop=True).then_inc(pro_mm, 1)
            pe.wait_ge(pro_v, 6)
            for c in range(FC):
                last = te.matmul(small[:, 0, c * D:(c + 1) * D], lora_2[:, c * P:(c + 1) * P], lora_d,
                                 start=True, stop=True)
            last.then_inc(pro_mm, 1)
            pe.wait_ge(pro_v, 7)

            with pe.Fori(0, B) as it:
                for layer in range(LAYERS):
                    call = it * LAYERS + layer
                    groups = call * NG

                    def norm_turns(which):
                        pe.wait_ge(xn_ready, it * 4 + layer * 2 + which + 1)
                        for fc in range(FC):
                            turn = first_turn["norm" if which == 0 else "norm2", layer] + fc
                            wait_half(pe, it, turn)
                            for t in range(NT):
                                last = te.transpose(big[:, turn % 2, t * P:(t + 1) * P], xn[:, t, fc * P:(fc + 1) * P],
                                                    ident[:])
                            last.then_inc(filled, 1)

                    def feature_turn(turn, w, rhs, ft):
                        wait_half(pe, it, turn)
                        for tb in range(2):
                            for c in range(FC):
                                last = te.matmul(big[:, turn % 2, tb * BANK:(tb + 1) * BANK],
                                                 w[:, c, ft * P:(ft + 1) * P], rhs[:, c, tb * BANK:(tb + 1) * BANK],
                                                 start=(c == 0), stop=(c == FC - 1))
                        last.then_inc(filled, 1)

                    def token_turn(turn, lhs, w, chunks, n):
                        wait_half(pe, it, turn)
                        for t in range(4):
                            for c in range(chunks):
                                last = te.matmul(big[:, turn % 2, t * D:(t + 1) * D],
                                                 lhs[:, c, (n * 4 + t) * P:(n * 4 + t + 1) * P], w[:, c, :],
                                                 start=(c == 0), stop=(c == chunks - 1))
                        last.then_inc(filled, 1)

                    norm_turns(0)
                    h_all = hT[:, :, 1:]
                    wait_emptied(pe, it, first_turn["norm", layer])
                    wait_emptied(pe, it, first_turn["norm", layer] + 1)
                    pe.wait_ge(w_loaded, call * 16 + 16)
                    for ft in range(FC):
                        for w in range(2):
                            feature_turn(first_turn["qk", layer] + 2 * ft + w, w_qkv[:, w], h_all, ft)
                    if layer == 1:
                        for ft in range(FC):
                            for w in range(2):
                                wait_emptied(pe, it, first_turn["qk", 1] + 2 * ft + w)
                                turn = first_turn["rope", 1] + 2 * ft + w
                                wait_half(pe, it, turn)
                                for tb in range(2):
                                    last = te.matmul(big[:, turn % 2, tb * BANK:(tb + 1) * BANK], perm_sb[:],
                                                     qk32[:, w, ft, tb * BANK:(tb + 1) * BANK], start=True, stop=True)
                                last.then_inc(filled, 1)
                    for n in range(2):
                        token_turn(first_turn["v", layer] + n, h_all, w_qkv[:, 2], FC, n)

                    def max_step(n):
                        step = MAX_STEPS[n]
                        pe.wait_ge(s_freed, call * len(MAX_STEPS) + n + 1)
                        if step[0] == "max":
                            _, g, h, qt, half = step
                            if h == 0 and qt == 0 and half == 0 and g % 2 == 0:
                                pe.wait_ge(stacked[g // 2], call * 128 + 128)
                                if g == 0:
                                    pe.wait_ge(rows_loaded, call * 32 + 32)
                            head = g * GH + h
                            k0 = half * BANK
                            k1 = (qt + 1) * P if half or qt < NT // 2 else BANK
                            te.matmul(small[:, n % 2, 0:k1 - k0], stack_q[:, head, qt * P:(qt + 1) * P],
                                      stack_k[:, head, k0:k1], start=True, stop=True).then_inc(s_filled, 1)
                        else:
                            g = step[1]
                            pe.wait_ge(max_ready, groups + g + 1)
                            te.transpose(small[0:GH * NT, n % 2, 0:P], mxc[:, g % 2, :], ident[:]).then_inc(s_filled, 1)

                    def score_turn(g, i):
                        kt, heads = SCORE_TURNS[i]
                        turn = first_turn["score", layer] + g * len(SCORE_TURNS) + i
                        if i == 0:
                            pe.wait_ge(mrow_loaded[g % 2], (call * 2 + g // 2) * 32 + 32)
                        wait_half(pe, it, turn)
                        for j, h in enumerate(heads):
                            q0 = kt * P
                            while q0 < T:
                                q1 = min(T, (q0 // BANK + 1) * BANK)
                                at = q0 if len(heads) == 1 else j * (HALF // len(heads))
                                last = te.matmul(big[:, turn % 2, at:at + q1 - q0],
                                                 stack_k[:, g * GH + h, kt * P:(kt + 1) * P],
                                                 stack_q[:, g * GH + h, q0:q1], start=True, stop=True)
                                q0 = q1
                        last.then_inc(filled, 1)

                    def context(g, kt, bank):
                        if bank == (kt * P) // BANK:
                            pe.wait_ge(masked, (groups + g) * NT + kt + 1)
                            if kt == 0 and g:
                                pe.wait_ge(ctx_saved, groups + g)
                        q0, q1 = max(kt * P, bank * BANK), (bank + 1) * BANK
                        for h in range(GH):
                            last = te.matmul(ctx_ps[32 * h:32 * (h + 1), q0:q1], v_ones[:, kt, g * GH + h, :],
                                             probs[:, kt % 2, h, q0:q1], start=(kt == 0), stop=(kt == q1 // P - 1))
                        if bank == T // BANK - 1:
                            last.then_inc(pv_done, 1)

                    for n in range(LEAD):
                        max_step(n)
                    sent, spent = LEAD, 0.0
                    for item in MAIN_ITEMS:
                        if item[0] == "score":
                            score_turn(*item[1:])
                        else:
                            context(*item[1:])
                        spent += item_columns(item)
                        while sent < len(MAX_STEPS) and STEP_END[sent] - STEP_END[LEAD - 1] <= spent * PACE:
                            max_step(sent)
                            sent += 1
                    while sent < len(MAX_STEPS):
                        max_step(sent)
                        sent += 1

                    pe.wait_ge(w_scaled, call * 2 + 1)
                    pe.wait_ge(ctx_ready, groups + NG + 1)
                    for n in range(2):
                        token_turn(first_turn["proj", layer] + n, ctxT, w_out_g, NG, n)
                    norm_turns(1)
                    if layer == 0:
                        for n in range(2):
                            if n == 0:
                                pe.wait_ge(mix_ready, it * 4 + 2)
                            token_turn(first_turn["r", 0] + n, mix_r, w_ffn[:, 0], FC, n)
                        pe.wait_ge(mix_ready, it * 4 + 4)
                        for ft in range(FC):
                            feature_turn(first_turn["k", 0] + ft, w_ffn[:, 1], mix_k, ft)
                        pe.wait_ge(act_ready, it * 2 + 2)
                        pe.wait_ge(w_scaled, call * 2 + 2)
                        for n in range(2):
                            token_turn(first_turn["y", 0] + n, k_act, w_last_g, FC, n)
                    else:
                        wait_emptied(pe, it, first_turn["norm2", 1])
                        wait_emptied(pe, it, first_turn["norm2", 1] + 1)
                        pe.wait_ge(w_scaled, call * 2 + 2)
                        for n in range(2):
                            token_turn(first_turn["y", 1] + n, hT[:, :, 1:], w_last_g, FC, n)


def shape_constants():
    slopes = (2.0 ** (-8.0 * np.arange(1, H + 1, dtype=np.float32) / np.float32(H))).astype(np.float32)
    pos = np.arange(T, dtype=np.float32)
    rest = (slopes[:, None] * pos[None, :] * np.float32(SCALE)).astype(np.float32)
    alibi = np.zeros((N_ALIBI, H, T), np.float16)
    for n in range(N_ALIBI):
        alibi[n] = rest.astype(np.float16)
        rest = rest - alibi[n].astype(np.float32)
    zero = np.zeros((N_ALIBI, H, T), np.float16)
    one = np.ones((N_ALIBI, H, T), np.float16)
    unit = np.full((N_MAX, H, T), MAX_UNIT, np.float16)
    inv = (1.0 / np.float32(10000.0) ** (np.arange(0, DH, 2, dtype=np.float32) / np.float32(DH))).astype(np.float32)
    freqs = np.outer(pos, inv).astype(np.float32)
    emb = np.concatenate([freqs, freqs], axis=-1)
    cos = np.ascontiguousarray(np.tile(np.cos(emb).astype(np.float32).T, (HPT, 1)))
    sin = np.ascontiguousarray(np.tile(np.sin(emb).astype(np.float32).T, (HPT, 1)))
    perm = np.zeros((P, P), np.float32)
    for h in range(HPT):
        for d in range(DH // 2):
            perm[h * DH + d + DH // 2, h * DH + d] = -1.0
            perm[h * DH + d, h * DH + d + DH // 2] = 1.0
    return alibi, zero, one, unit, perm, cos, sin


def padded_heads(w):
    out = np.zeros((H, 2 * DH, w.shape[1]), w.dtype)
    out[:, :DH] = w.reshape(H, DH, -1)
    return out.reshape(H * 2 * DH, -1)


def kernel(**inputs):
    import concourse.bacc as bacc
    from concourse.bass_utils import run_bass_kernel_spmd

    a = {k: np.asarray(v) for k, v in inputs.items()}
    alibi, zero, one, unit, perm, cos, sin = shape_constants()
    arrays = {
        "x": a["L0_attn_x"],
        "c0": a["L0_c"].T, "c1": a["L1_c"].T, "wmod0": a["L0_wmod"], "wmod1": a["L1_wmod"],
        "wqkv": np.stack([np.stack([a["L0_attn_W_query"], a["L0_attn_W_key"], a["L0_attn_W_value"]]),
                          np.stack([a["L1_attn_Wq"].T, a["L1_attn_Wk"].T, a["L1_attn_Wv"].T])]),
        "wout": np.stack([padded_heads(a["L0_attn_W_proj"]), padded_heads(a["L1_attn_Wo"].T)]),
        "bias": np.stack([a["L0_attn_b_proj"], a["L1_ffn_b"]]),
        "wffn": np.stack([a["L0_ffn_W_r"].T, a["L0_ffn_W_k"].T, a["L0_ffn_W_v"].T]),
        "mu": np.stack([a["L0_ffn_mu_r"], a["L0_ffn_mu_k"]]).reshape(2 * FC, P).T,
        "down_t": a["L1_ffn_lora_down"].T, "down_aux": a["L1_ffn_down_aux"],
        "up_t": a["L1_ffn_lora_up"].T, "up_aux_t": a["L1_ffn_up_aux"].T,
        "wbase": a["L1_ffn_W"].T,
        "perm": perm, "cos": cos, "sin": sin,
        "alibi": alibi, "zero": zero, "one": one, "unit": unit,
    }
    arrays = {k: np.ascontiguousarray(v) for k, v in arrays.items()}
    nc = bacc.Bacc("TRN2", target_bir_lowering=False, num_devices=1)
    ap = {k: nc.dram_tensor(k, v.shape, mybir.dt.from_np(v.dtype), kind="ExternalInput").ap() for k, v in arrays.items()}
    out = nc.dram_tensor("out", (B, T, D), mybir.dt.float32, kind="ExternalOutput").ap()
    adaln_program(nc, ap["x"], ap["c0"], ap["c1"], ap["wmod0"], ap["wmod1"], ap["wqkv"], ap["wout"], ap["bias"],
                  ap["wffn"], ap["mu"], (ap["down_t"], ap["down_aux"], ap["up_t"], ap["up_aux_t"]), ap["wbase"],
                  (ap["perm"], ap["cos"], ap["sin"]), (ap["alibi"], ap["zero"], ap["one"], ap["unit"]), out)
    r = run_bass_kernel_spmd(nc, [arrays], core_ids=[0])
    return r.results[0]["out"]
```

```python
import numpy as np

import concourse.bass as bass
from concourse import mybir
from contextlib import ExitStack

B, T, D = 8, 1024, 256
H, DH = 16, 16
P = 128
NT = T // P
FC = D // P
GH = 4
NG = H // GH
HPT = P // DH
BANK = 512
RING = 3
BLOCKS = T // BANK
HH = H // 2
LAYERS = 2
EPS = 1e-5
SCALE = 0.25
NEG = -1e30

Q_PARTS = (0, 0, 1, 1)
K_PARTS = (0, 1, 0, 1)
ROW_ALIBI = len(Q_PARTS) * DH
N_ALIBI = 3
ROW_MAX = ROW_ALIBI + N_ALIBI
N_MAX = 2
MAX_UNIT = 64.0
K_USED = ROW_MAX + N_MAX


UNITS = ((0, 0), (1, 0), (0, 1), (1, 1))
PAIRS = B // 2


def block_tiles(blk):
    return [(kt, max(0, kt * P - blk * BANK)) for kt in range((blk + 1) * BANK // P)]


def is_diagonal(blk, kt):
    return kt >= blk * (BANK // P)


def score_turns(blk):
    out = []
    for kt, q0 in block_tiles(blk):
        n = {512: 1, 384: 1, 256: 2, 128: 4}[BANK - q0]
        out += [(kt, q0, tuple(range(h, h + n))) for h in range(0, GH, n)]
    return out


def attention_items():
    turns = [(g, blk, *t) for g in range(NG) for blk in range(BLOCKS) for t in score_turns(blk)]
    after = {}
    items, at = [], 0.0
    for n in range(len(turns) + 8):
        if n < len(turns):
            g, blk, kt, q0, heads = turns[n]
            items.append((at, ("score", g, blk, kt, q0, heads)))
            at += len(heads) * (BANK - q0)
            if n + 1 == len(turns) or turns[n + 1][:3] != turns[n][:3]:
                if is_diagonal(blk, kt):
                    items.append((at, ("mask", g, blk, kt, q0)))
                after.setdefault(n + LAG, []).append(("context", g, blk, kt, q0))
                if kt == (blk + 1) * BANK // P - 1:
                    after.setdefault(n + LAG + 1, []).append(("save", g, blk))
                    after.setdefault(n + LAG + 2, []).append(("norm", g, blk))
        for item in after.get(n, []):
            items.append((at, item))
            if item[0] == "context":
                at += 4 * (BANK - item[4])
    return [(p / at, i) for p, i in items]


LAG = 3


def max_steps():
    steps = []
    for g in range(NG):
        own = [("max", g, h, qt, blk) for h in range(GH) for qt in range(NT) for blk in range(qt // 4 + 1)]
        if g:
            own.insert(3, ("rows", g - 1))
        steps += own
    steps.append(("rows", NG - 1))
    return steps


MAX_STEPS = max_steps()
MAX_N = len([s for s in MAX_STEPS if s[0] == "max"]) // NG
LEAD = MAX_N + 8


def step_cost(step):
    if step[0] == "rows":
        return 350
    return 80 + (BANK if step[3] // 4 > step[4] else (step[3] % 4 + 1) * P)


def max_items(slot):
    steps = [(slot, s) for s in MAX_STEPS[LEAD:]] + [((slot + 1) % 4, s) for s in MAX_STEPS[:LEAD]]
    total = sum(step_cost(s) for _, s in steps)
    items, at = [], 0.0
    for unit, s in steps:
        items.append((at / total * MAX_SPREAD, (s[0], unit, *s[1:])))
        at += step_cost(s)
    return items


def spread(start, end, items):
    return [(start + (end - start) * n / len(items), i) for n, i in enumerate(items)]


def post_items(unit, at):
    layer = UNITS[unit][1]
    proj = [("proj", unit, n) for n in range(4)]
    norm = [("ln", unit, 1, n) for n in range(5)]
    turned = [("turned", unit, 1, fc, tb) for fc in range(FC) for tb in range(2)]
    items = [(0.002, ("scale", unit, 0))]
    if layer == 0:
        items += spread(0.004, 0.06, [("bias", unit, n) for n in range(4)])
    items += spread(at["proj"][0], at["proj"][1], proj)
    items += spread(at["ln2"][0], at["ln2"][1], norm)
    items += spread(at["turn2"][0], at["turn2"][1], turned)
    items += [(at["turn2"][0], ("scale", unit, 1))]
    if layer == 0:
        items += spread(*at["mix"], [("mix", unit, fc, tb) for fc in range(FC) for tb in range(2)])
        k, s = ([(kind, unit, ft, tb) for ft in range(FC) for tb in range(2)] for kind in ("key", "square"))
        items += spread(*at["ffn"], [("gate", unit, n) for n in range(4)] + [*k[:3], s[0], k[3], *s[1:]])
        items += spread(*at["y0"], [("y", unit, n) for n in range(4)])
        items += [(at["y0"][1] + 0.002, ("post_loads", (unit + 1) % 4))]
    else:
        items += spread(*at["bias2"], [("bias", unit, n) for n in range(4)])
        items += spread(*at["y1"], [("y", unit, n) for n in range(4)])
        items += [(at["y1"][1] + 0.003, ("store", unit)), (at["y1"][1] + 0.002, ("post_loads", (unit + 1) % 4)),
                  (at["y1"][1] + 0.004, ("x_load", (unit + 2) % 4))]
    return items


def pre_items(unit, at):
    layer = UNITS[unit][1]
    items = [(at["v1"] + 0.01, ("pre_loads", unit))]
    items += spread(*at["ln1"], [("ln", unit, 0, n) for n in range(5)])
    items += spread(*at["turn1"], [("turned", unit, 0, fc, tb) for fc in range(FC) for tb in range(2)])
    for ft in range(FC):
        q, r, s = ([(k, unit, ft, w, tb) for w in range(2) for tb in range(2)] for k in ("qk", "rope", "split"))
        qk = [*q[:3], s[0], q[3], *s[1:]]
        if layer:
            qk = [*q[:3], r[0], q[3], r[1], s[0], r[2], s[1], r[3], *s[2:]]
        items += spread(*at[f"qk{ft}"], qk)
        items += [(at[f"qk{ft}"][1] + 0.01, ("parts_save", unit, ft))]
    items += [(at["stack0"], ("stack_load", unit, 0))]
    items += spread(*at["v0"], [("value", unit, 0, n) for n in range(2)])
    return items


AT = {"v1": 0.05, "proj": (0.085, 0.135), "ln2": (0.145, 0.18), "turn2": (0.195, 0.22), "mix": (0.23, 0.26),
      "ffn": (0.27, 0.37), "y0": (0.39, 0.43), "bias2": (0.20, 0.24), "y1": (0.25, 0.33),
      "ln1": (0.455, 0.49), "turn1": (0.505, 0.53), "qk0": (0.54, 0.63), "stack0": 0.655, "qk1": (0.66, 0.78),
      "v0": (0.80, 0.86)}
MAX_SPREAD = 1.0


def slot_items(slot):
    before, behind = (slot - 1) % 4, (slot + 1) % 4
    items = attention_items() + max_items(slot)
    items += [(0.03, ("stack_load", slot, 1))] + spread(AT["v1"], AT["v1"] + 0.01, [("value", slot, 1, n) for n in range(2)])
    items += post_items(before, AT) + pre_items(behind, AT)
    return [i for _, i in sorted(items, key=lambda x: x[0])]


FIRST_ITEMS = [i for _, i in sorted([x for x in pre_items(0, AT)], key=lambda x: x[0])] + \
    [(s[0], 0, *s[1:]) for s in MAX_STEPS[:LEAD]]
FIRST_ITEMS = [("post_loads", 3), ("x_load", 0)] + FIRST_ITEMS
LOOP_ITEMS = [(slot, i) for slot in range(4) for i in slot_items(slot)]
LAST_ITEMS = [i for _, i in sorted(post_items(3, AT), key=lambda x: x[0]) if i[0] not in ("post_loads", "x_load")]

TURN_KINDS = ("score", "rows", "proj", "turned", "gate", "key", "y", "qk", "rope", "value")


def events(item):
    kind = item[0]
    e = {"item": 1, kind: 1}
    if kind in TURN_KINDS:
        e["turn"] = 1
    if kind == "rows":
        e[f"rows_{item[2] % 2}"] = 1
    if kind == "stack_load":
        e[f"stack_{item[2]}"] = 1
    if kind == "ln" and item[3] == 4:
        e["normed"] = 1
    if kind == "norm" and item[1] % 2:
        e["ctx_ready"] = 1
    if kind == "split" and UNITS[item[1]][1]:
        e["rope_split"] = 1
    if kind == "x_load":
        e[f"x_{UNITS[item[1]][0]}"] = 1
    if kind == "ln" and item[2:] == (0, 0) and UNITS[item[1]][1]:
        e["tables"] = 1
    return e


def totals(items):
    sums = {}
    for i in items:
        for k, n in events(i).items():
            sums[k] = sums.get(k, 0) + n
    return sums


FIRST = totals(FIRST_ITEMS)
EACH = totals([i for _, i in LOOP_ITEMS])
assert EACH["turn"] % RING == 0 and EACH["max"] % RING == 0 and EACH["context"] % RING == 0
V_CHAIN = (28, 288)
CONTEXTS = NG * sum(len(block_tiles(blk)) for blk in range(BLOCKS))


def context_number(slot, g, blk, kt):
    return slot * CONTEXTS + g * (CONTEXTS // NG) + (len(block_tiles(0)) if blk else 0) + kt


class Place:

    def __init__(self, section, it=None):
        self.section, self.it, self.counts, self.turns = section, it, {}, {}

    def base(self, kind, first=None, each=None):
        first = FIRST.get(kind, 0) if first is None else first
        each = EACH.get(kind, 0) if each is None else each
        return {"first": lambda: 0, "loop": lambda: self.it * each + first,
                "last": lambda: PAIRS * each + first}[self.section]()

    def own(self, kind):
        return self.counts.get(kind, 0)

    def now(self, kind, more=0, unit=1):
        if self.section == "loop":
            return self.it * (EACH.get(kind, 0) * unit) + (FIRST.get(kind, 0) + self.own(kind) + more) * unit
        return (self.base(kind) + self.own(kind) + more) * unit

    def turn(self):
        return self.own("turn")

    def slot(self, turn=None):
        turn = self.turn() if turn is None else turn
        return (turn if self.section == "first" else FIRST["turn"] + turn) % RING

    def uses(self, turn):
        if self.section == "first":
            return turn // RING
        n = (FIRST["turn"] + turn) // RING
        return (self.it * (EACH["turn"] // RING) if self.section == "loop" else PAIRS * (EACH["turn"] // RING)) + n

    def small(self):
        return (self.own("max") + (0 if self.section == "first" else FIRST["max"])) % RING

    def loops(self, each):
        return self.it * each

    def done(self, item):
        if item[0] in TURN_KINDS:
            self.turns[item] = self.turn()
            if item[0] == "score":
                self.turns[item[:4]] = self.turn()
        for k, n in events(item).items():
            self.counts[k] = self.counts.get(k, 0) + n

    def batch(self, unit, slot, post):
        if self.section != "loop":
            return B - 1 if post else 0
        stream = UNITS[unit][0]
        if post and slot == 0:
            return (self.it * 2 + (B - 1)) % B
        if not post and slot == 3:
            return (self.it * 2 + 2) % B
        return self.it * 2 + stream


def adaln_program(nc, x, c0, c1, wmod0, wmod1, wqkv, wout, bias, wffn, mu, lora, wbase, rope, rows_c, out):
    f32, f16, bf16, i32 = mybir.dt.float32, mybir.dt.float16, mybir.dt.bfloat16, mybir.dt.int32
    ALU = mybir.AluOpType
    ACT = mybir.ActivationFunctionType
    AX = mybir.AxisListType.X
    down_t, down_aux, up_t, up_aux_t = lora
    perm, cos, sin = rope
    alibi_rows, zero_rows, one_rows, unit_rows = rows_c

    parts_dram = nc.dram_tensor("parts_dram", (2, FC, 2, P, T), f16, kind="Internal").ap()
    gate_dram = nc.dram_tensor("gate_dram", (B, LAYERS, 2 * D), f32, kind="Internal").ap()
    weff_dram = nc.dram_tensor("weff_dram", (P, FC * D), f32, kind="Internal").ap()

    ctx = ExitStack()
    with ctx:
        def sb(name, shape, dt=f32):
            return ctx.enter_context(nc.sbuf_tensor(name, shape, dt))

        def sem(name):
            return ctx.enter_context(nc.semaphore(name))

        x_res = sb("x_res", [P, 2, NT, D])
        xn = sb("xn", [P, NT, D])
        hT = sb("hT", [P, FC, T + 1])
        stack_q = sb("stack_q", [P, H, T], f16)
        stack_k = sb("stack_k", [P, H, T], f16)
        v_ones = sb("v_ones", [P, NT, H, DH + 1])
        probs = sb("probs", [P, RING, GH, BANK])
        ctx_u = sb("ctx_u", [P, BLOCKS, BANK])
        ctx_b = sb("ctx_b", [P, BANK])
        ctx_n = sb("ctx_n", [P, BLOCKS, BANK])
        ctxT = sb("ctxT", [P, NG // 2, T])
        region = sb("region", [P, 8 * T])
        mask = sb("mask", [P, BANK], bf16)
        mx = sb("mx", [P, 2, GH * NT, 2])
        mxc = sb("mxc", [P, 2, GH * NT])
        m_hi = sb("m_hi", [GH * NT, 2, P], f16)
        m_lo = sb("m_lo", [GH * NT, 2, P], f16)
        w_qkv = sb("w_qkv", [P, 3, FC, D])
        w_out = sb("w_out", [P, NG // 2, D])
        w_ffn = sb("w_ffn", [P, 3, FC, D])
        gates = sb("gates", [P, 2, D])
        bias_bc = sb("bias_bc", [P, D])
        modT = sb("modT", [P, 16, B])
        modc = sb("modc", [P, 2, 8])
        mu_c = sb("mu_c", [P, 2, FC])
        ident = sb("ident", [P, P])
        perm_sb = sb("perm_sb", [P, P])
        stats = sb("stats", [P, NT, 6])
        mv = sb("mv", [P, NT, 2])
        ve = sb("ve", [P, NT])
        rstd = sb("rstd", [P, NT])
        tmp = sb("tmp", [P, NT])
        nmr = sb("nmr", [P, NT])
        qk32 = region[:, 0:2 * T].rearrange("p (w t) -> p w t", w=2)
        parts = region[:, 2 * T:4 * T].bitcast(f16).rearrange("p (w s t) -> p w s t", w=2, s=2)
        rope_sin = region[:, 4 * T:5 * T].rearrange("p (a t) -> p a t", a=2)
        rope_cos = region[:, 5 * T:6 * T].rearrange("p (a t) -> p a t", a=2)
        cos_sb = region[:, 6 * T:7 * T]
        sin_sb = region[:, 7 * T:8 * T]
        mix_r = region[:, 0:2 * T].rearrange("p (f t) -> p f t", f=FC)
        mix_k = region[:, 2 * T:4 * T].rearrange("p (f t) -> p f t", f=FC)
        k_act = region[:, 4 * T:6 * T].rearrange("p (f t) -> p f t", f=FC)
        r_gate = region[:, 6 * T:8 * T].rearrange("p (t n) -> p t n", t=NT)
        v_prod = xn
        wmod_sb = region[:, 0:6 * T].rearrange("p (l c n) -> p l c n", l=2, c=FC)
        silu_in = ctx_b[:, 0:32].rearrange("p (l c b) -> p l c b", l=2, c=FC)
        silu_e = ctx_b[:, 32:64].rearrange("p (l c b) -> p l c b", l=2, c=FC)
        silu_o = ctx_b[:, 64:96].rearrange("p (l c b) -> p l c b", l=2, c=FC)
        gate_raw = x_res[0:B, 0, 0:4, :].rearrange("b t n -> b (t n)")
        gate_neg = x_res[0:B, 0, 4:8, :].rearrange("b t n -> b (t n)")
        gate_abs = x_res[0:B, 1, 0:4, :].rearrange("b t n -> b (t n)")
        gate_sgn = x_res[0:B, 1, 4:8, :].rearrange("b t n -> b (t n)")
        room = xn[:].rearrange("p t n -> p (t n)")
        lora_a = room[0:100, 0:4]
        lora_b = room[0:100, 8:8 + D]
        lora_c = room[0:4, 272:322]
        lora_d = room[0:50, 328:328 + D]
        lora_1 = room[0:4, 592:592 + D]
        lora_2 = room[0:50, 856:856 + D]
        w_lin = w_ffn[:, 2]

        big = ctx.enter_context(nc.psum_tensor("big", [P, RING, BANK], f32))
        ctx_ps = ctx.enter_context(nc.psum_tensor("ctx_ps", [P, BLOCKS, BANK], f32))
        small = ctx.enter_context(nc.psum_tensor("small", [P, RING, BANK], f32))

        consts_in = sem("consts_in")
        consts_set = sem("consts_set")
        stacks_clear = sem("stacks_clear")
        silu_exp = sem("silu_exp")
        pro_mm = sem("pro_mm")
        pro_v = sem("pro_v")
        gates_out = sem("gates_out")
        x_loaded = [sem("x_loaded_0"), sem("x_loaded_1")]
        post_loaded = sem("post_loaded")
        pre_loaded = sem("pre_loaded")
        tables_loaded = sem("tables_loaded")
        filled = sem("filled")
        freed = [sem(f"freed_{i}") for i in range(RING)]
        s_filled = sem("s_filled")
        s_freed = sem("s_freed")
        xn_ready = sem("xn_ready")
        modc_ready = sem("modc_ready")
        split_done = sem("split_done")
        parts_saved = sem("parts_saved")
        stacked = [sem("stacked_0"), sem("stacked_1")]
        rope_cos_ready = sem("rope_cos_ready")
        max_ready = sem("max_ready")
        rows_sent = [sem("rows_sent_0"), sem("rows_sent_1")]
        masked = sem("masked")
        pv_done = sem("pv_done")
        ctx_saved = sem("ctx_saved")
        u_read = sem("u_read")
        ctx_ready = sem("ctx_ready")
        scaled = sem("scaled")
        bias_gated = sem("bias_gated")
        biased = sem("biased")
        mixed = sem("mixed")
        squared = sem("squared")
        y_added = sem("y_added")
        stored = sem("stored")
        v_chain = sem("v_chain")
        g_chain = sem("g_chain")
        waits_taken = sem("waits_taken")

        def settle(eng):
            eng.sem_inc(waits_taken, 1)

        def wait_filled(eng, at):
            eng.wait_ge(filled, at.now("turn", 1))

        def wait_bank(eng, at):
            eng.wait_ge(freed[at.slot()], at.uses(at.turn()) + 1)

        def wait_emptied(eng, at, turn):
            eng.wait_ge(freed[at.slot(turn)], at.uses(turn) + 2)

        def sections(eng, step):
            at = Place("first")
            for item in FIRST_ITEMS:
                step(at, 3, item)
                at.done(item)
            with eng.Fori(0, PAIRS) as it:
                at = Place("loop", it)
                for slot, item in LOOP_ITEMS:
                    step(at, slot, item)
                    at.done(item)
            at = Place("last")
            for item in LAST_ITEMS:
                step(at, 0, item)
                at.done(item)

        n_consts = 15
        block = ctx.enter_context(nc.Block())

        @block.sync
        def _(sp):
            def load(dst, src):
                sp.dma_start(dst, src).then_inc(consts_in, 16)

            for l, (c, w) in enumerate(((c0, wmod0), (c1, wmod1))):
                load(silu_in[:, l], c.rearrange("(c p) b -> p c b", p=P))
                load(wmod_sb[:, l], w.rearrange("(c p) n -> p c n", p=P))
            load(w_lin, wbase.rearrange("(c p) n -> p c n", p=P))
            load(lora_a, down_t)
            load(lora_b, down_aux)
            load(lora_c, up_t)
            load(lora_d, up_aux_t)
            load(mu_c[:].rearrange("p w c -> p (w c)"), mu)
            load(perm_sb[:], perm)
            sp.wait_ge(stacks_clear, 2)
            for half in range(2):
                heads = slice(half * HH, (half + 1) * HH)
                load(stack_q[ROW_ALIBI:ROW_MAX, heads], one_rows[:, heads])
                load(stack_k[ROW_MAX:K_USED, heads], unit_rows[:, heads])
            sp.wait_ge(pro_v, 7)
            sp.dma_start(gate_dram.rearrange("b l n -> b (l n)"), gate_raw).then_inc(gates_out, 16)
            sp.dma_start(weff_dram, w_lin.rearrange("p c n -> p (c n)")).then_inc(gates_out, 16)
            sp.wait_ge(gates_out, 32)
            sp.wait_ge(pro_v, 8)

            marks = {}

            def step(at, slot, item):
                kind, unit = item[0], item[1]
                stream, layer = UNITS[unit] if unit < 4 else (0, 0)
                if kind == "post_loads":
                    if at.section != "first":
                        sp.wait_ge(y_added, at.now("y"))
                        settle(sp)
                    b = at.it * 2 + stream if at.section == "loop" else B - 1
                    src = wout[layer].rearrange("(g p) n -> p g n", p=P)
                    sp.dma_start(w_out[:], src).then_inc(post_loaded, 16)
                    if layer == 0:
                        sp.dma_start(w_ffn[:], wffn.rearrange("w (c p) n -> p w c n", p=P)).then_inc(post_loaded, 16)
                    else:
                        sp.dma_start(w_lin, weff_dram.rearrange("p (c n) -> p c n", c=FC)).then_inc(post_loaded, 16)
                    gsrc = gate_dram[b:b + 1, layer] if isinstance(b, int) else \
                        gate_dram[bass.ds(b, 1), layer]
                    sp.dma_start(gates[:].rearrange("p g n -> p (g n)"), gsrc.broadcast_to([P, 2 * D]))\
                        .then_inc(post_loaded, 16)
                    sp.dma_start(bias_bc[:], bias[layer:layer + 1, :].broadcast_to([P, D])).then_inc(post_loaded, 16)
                elif kind == "pre_loads":
                    if at.section != "first":
                        sp.wait_ge(filled, at.now("turn"))
                    sp.dma_start(w_qkv[:], wqkv[layer].rearrange("w (c p) n -> p w c n", p=P)).then_inc(pre_loaded, 16)
                elif kind == "ln" and item[2] == 0 and item[3] == 0 and layer == 1:
                    sp.wait_ge(y_added, at.now("y"))
                    sp.dma_start(cos_sb, cos).then_inc(tables_loaded, 16)
                    sp.dma_start(sin_sb, sin).then_inc(tables_loaded, 16)
                elif kind == "parts_save":
                    ft = item[2]
                    sp.wait_ge(split_done, at.now("split"))
                    for w in range(2):
                        sp.dma_start(parts_dram[w, ft].rearrange("s p t -> p s t"), parts[:, w])\
                            .then_inc(parts_saved, 16)
                    sp.wait_ge(parts_saved, at.now("parts_save", 1, 32))
                    settle(sp)
                elif kind == "stack_load":
                    half = item[2]
                    if at.section != "first":
                        sp.wait_ge(filled, at.now("turn"))
                    for w, (stack, order) in enumerate(((stack_q, Q_PARTS), (stack_k, K_PARTS))):
                        for r, s in enumerate(order):
                            sp.dma_start(stack[r * DH:(r + 1) * DH, half * HH:(half + 1) * HH, :],
                                         parts_dram[w, half, s].rearrange("(h d) t -> d h t", d=DH))\
                                .then_inc(stacked[half], 16)
                    heads = slice(half * HH, (half + 1) * HH)
                    sp.dma_start(stack_k[ROW_ALIBI:ROW_MAX, heads], (zero_rows if layer else alibi_rows)[:, heads])\
                        .then_inc(stacked[half], 16)
                    sp.dma_start(stack_q[ROW_MAX:K_USED, heads], zero_rows[0:N_MAX, heads]).then_inc(stacked[half], 16)
                elif kind == "rows":
                    g = item[2]
                    wait_emptied(sp, at, at.turn())
                    for r, m in enumerate((m_hi, m_lo)):
                        sp.dma_start(stack_q[ROW_MAX + r:ROW_MAX + r + 1, g * GH:(g + 1) * GH, :]
                                     .rearrange("r h (q t) -> r (h q) t", t=P), m[:, g % 2, :])\
                            .then_inc(rows_sent[g % 2], 16)
                elif kind == "store":
                    sp.wait_ge(y_added, at.now("y"))
                    settle(sp)
                    b = at.batch(unit, slot, True)
                    dst = out[b] if isinstance(b, int) else out[bass.ds(b, 1)].rearrange("o n d -> (o n) d")
                    sp.dma_start(dst.rearrange("(t p) n -> p t n", p=P), x_res[:, stream]).then_inc(stored, 16)
                elif kind == "x_load":
                    if at.section != "first":
                        sp.wait_ge(stored, at.now("store", 0, 16))
                        settle(sp)
                    b = at.batch(unit, slot, False)
                    src = x[b] if isinstance(b, int) else x[bass.ds(b, 1)].rearrange("o n d -> (o n) d")
                    sp.dma_start(x_res[:, stream], src.rearrange("(t p) n -> p t n", p=P)).then_inc(x_loaded[stream], 16)

            sections(sp, step)
            sp.wait_ge(stored, 16 * (PAIRS * 2 + 1))
            sp.wait_ge(x_loaded[0], 16 * (PAIRS + 1))

        @block.gpsimd
        def _(pool):
            g = nc.gpsimd
            g.memset(ident[:], 0.0).then_inc(g_chain, 1)
            g.memset(mask[:], 0.0).then_inc(g_chain, 1)
            g.memset(v_ones[:], 1.0).then_inc(consts_set, 1)
            pool.wait_ge(g_chain, 2)
            g.affine_select(out=ident[:], in_=ident[:], compare_op=ALU.not_equal, fill=1.0, base=0,
                            pattern=[[-1, P]], channel_multiplier=1).then_inc(consts_set, 1)
            g.affine_select(out=mask[:, BANK - P:], in_=mask[:, BANK - P:], compare_op=ALU.is_ge, fill=NEG, base=0,
                            pattern=[[-1, P]], channel_multiplier=1).then_inc(consts_set, 1)
            pool.wait_ge(consts_in, 16 * n_consts)

            def step(at, slot, item):
                kind, unit = item[0], item[1]
                if kind == "mask":
                    _, g_, blk, kt, q0 = item
                    wait_emptied(pool, at, at.turns["score", g_, blk, kt])
                    settle(pool)
                    diag = probs[:, context_number(slot, g_, blk, kt) % RING, :, q0:q0 + P]
                    g.affine_select(out=diag, in_=diag, compare_op=ALU.is_ge, fill=0.0, base=0,
                                    pattern=[[0, GH], [1, P]], channel_multiplier=-1).then_inc(masked, 1)
                elif kind == "scale" and item[2] == 0:
                    layer = UNITS[unit][1]
                    pool.wait_ge(post_loaded, at.now("post_loads", 0, 64))
                    g.tensor_tensor(w_out[:], w_out[:], gates[:, 0:1, :].broadcast_to([P, NG // 2, D]), ALU.mult)\
                        .then_inc(scaled, 1)
                    g.tensor_tensor(bias_bc[:], bias_bc[:], gates[:, layer], ALU.mult).then_inc(bias_gated, 1)
                elif kind == "scale":
                    g.tensor_tensor(w_ffn[:, 2], w_ffn[:, 2], gates[:, 1:2, :].broadcast_to([P, FC, D]), ALU.mult)\
                        .then_inc(scaled, 1)
                elif kind == "bias":
                    stream, layer = UNITS[unit]
                    n = item[2]
                    if n == 0:
                        pool.wait_ge(bias_gated, at.now("post_loads", 0))
                        pool.wait_ge(xn_ready, at.now("normed"))
                    own = x_res[:, stream, 2 * n:2 * n + 2]
                    g.tensor_tensor(own, own, bias_bc[:].rearrange("p (o n) -> p o n", o=1).broadcast_to([P, 2, D]),
                                    ALU.add).then_inc(biased, 1)
                elif kind == "rope":
                    _, _, ft, w, tb = item
                    if ft == 0 and w == 0 and tb == 0:
                        pool.wait_ge(tables_loaded, at.now("tables", 0, 32))
                    n = at.own("rope")
                    wait_emptied(pool, at, at.turns["qk", unit, ft, w, tb])
                    pool.wait_ge(split_done, at.now("split"))
                    g.tensor_tensor(rope_cos[:, n % 2], qk32[:, w, tb * BANK:(tb + 1) * BANK],
                                    cos_sb[:, tb * BANK:(tb + 1) * BANK], ALU.mult).then_inc(rope_cos_ready, 1)

            sections(pool, step)

        @block.scalar
        def _(act):
            s = nc.scalar
            act.wait_ge(consts_in, 16 * n_consts)
            s.activation(silu_e, silu_in, ACT.Exp, scale=-1.0).then_inc(silu_exp, 1)

            def step(at, slot, item):
                kind, unit = item[0], item[1]
                if kind in TURN_KINDS and kind not in ("rows", "proj", "rope", "y"):
                    bank, emptied = big[:, at.slot(), :], freed[at.slot()]
                if kind == "score":
                    _, g, blk, kt, q0, heads = item
                    n = context_number(slot, g, blk, kt)
                    if heads[0] == 0:
                        act.wait_ge(pv_done, at.loops(4 * CONTEXTS) + n + 1)
                    wait_filled(act, at)
                    width = BANK - q0
                    s.activation(probs[:, n % RING, heads[0]:heads[-1] + 1, q0:],
                                 bank[:, 0:len(heads) * width].rearrange("p (h q) -> p h q", h=len(heads)), ACT.Exp)\
                        .then_inc(emptied, 1)
                elif kind == "save":
                    _, g, blk = item
                    n = slot * NG * BLOCKS + g * BLOCKS + blk
                    act.wait_ge(pv_done, at.loops(4 * CONTEXTS) + context_number(slot, g, blk, (blk + 1) * 4 - 1) + 1 + RING)
                    act.wait_ge(u_read, at.loops(4 * NG * BLOCKS) + n + 1)
                    s.activation(ctx_u[:, blk], ctx_ps[:, blk], ACT.Copy).then_inc(ctx_saved, 1)
                elif kind == "turned":
                    _, _, which, fc, tb = item
                    act.wait_ge(modc_ready, at.now("normed"))
                    wait_filled(act, at)
                    col = which * 2 + fc
                    s.activation(hT[:, fc, 1 + tb * BANK:1 + (tb + 1) * BANK], bank, ACT.Identity,
                                 scale=modc[:, which, col + 4:col + 5], bias=modc[:, which, col:col + 1])\
                        .then_inc(emptied, 1)
                elif kind == "qk":
                    _, _, ft, w, tb = item
                    if at.section != "first" or at.own("split"):
                        act.wait_ge(split_done, at.now("split"))
                    wait_filled(act, at)
                    s.activation(qk32[:, w, tb * BANK:(tb + 1) * BANK], bank, ACT.Copy, scale=SCALE if w == 0 else 1.0)\
                        .then_inc(emptied, 1)
                elif kind == "value":
                    _, _, half, n = item
                    wait_filled(act, at)
                    s.activation(v_ones[:, n * 4:(n + 1) * 4, half * HH:(half + 1) * HH, 0:DH],
                                 bank.rearrange("p (t h d) -> p t h d", t=4, h=HH), ACT.Copy).then_inc(emptied, 1)
                elif kind == "gate":
                    n = item[2]
                    wait_filled(act, at)
                    s.activation(r_gate[:, 2 * n:2 * n + 2, :], bank.rearrange("p (t n) -> p t n", t=2), ACT.Tanh,
                                 scale=0.5).then_inc(emptied, 1)
                elif kind == "key":
                    _, _, ft, tb = item
                    wait_filled(act, at)
                    s.activation(k_act[:, ft, tb * BANK:(tb + 1) * BANK], bank, ACT.Relu).then_inc(emptied, 1)

            sections(act, step)

        @block.vector
        def _(dve):
            v = nc.vector
            for stack in (stack_q, stack_k):
                v.memset(stack[P // 2:], 0.0).then_inc(stacks_clear, 1)
            for bank in freed:
                dve.sem_inc(bank, 1)
            dve.sem_inc(s_freed, RING)
            dve.sem_inc(pv_done, RING)
            dve.sem_inc(ctx_saved, BLOCKS)
            dve.sem_inc(u_read, BLOCKS)
            dve.wait_ge(consts_in, 16 * n_consts)
            dve.wait_ge(silu_exp, 1)
            v.tensor_scalar_add(silu_e, silu_e, 1.0).then_inc(pro_v, 1)
            dve.wait_ge(pro_v, 1)
            v.reciprocal(silu_e, silu_e).then_inc(pro_v, 1)
            dve.wait_ge(pro_v, 2)
            v.tensor_tensor(silu_o, silu_in, silu_e, ALU.mult).then_inc(pro_v, 1)
            dve.wait_ge(pro_mm, 1)
            v.tensor_copy(lora_1, small[0:4, 1, 0:D]).then_inc(pro_v, 1)
            dve.wait_ge(pro_mm, 2)
            v.tensor_copy(lora_2, small[0:50, 1, D:2 * D]).then_inc(pro_v, 1)
            dve.wait_ge(pro_mm, 3)
            v.tensor_tensor(w_lin, w_lin, small[:, 2, :].rearrange("p (c n) -> p c n", c=FC), ALU.add)\
                .then_inc(pro_v, 1)
            dve.wait_ge(pro_mm, 4)
            v.tensor_copy(gate_raw, ctx_ps[0:B].rearrange("b k n -> b (k n)")).then_inc(v_chain, 1)
            dve.wait_ge(v_chain, 1)
            v.tensor_scalar(gate_neg, gate_raw, -1.0, None, ALU.mult).then_inc(v_chain, 1)
            v.tensor_scalar(gate_sgn, gate_raw, 0.0, 2.0, ALU.is_ge, ALU.mult).then_inc(v_chain, 1)
            dve.wait_ge(v_chain, 3)
            v.tensor_tensor(gate_abs, gate_raw, gate_neg, ALU.max).then_inc(v_chain, 1)
            dve.wait_ge(v_chain, 4)
            v.tensor_scalar(gate_sgn, gate_sgn, -1.0, None, ALU.add).then_inc(v_chain, 1)
            v.tensor_scalar(gate_abs, gate_abs, 0.25, None, ALU.max).then_inc(v_chain, 1)
            dve.wait_ge(v_chain, 6)
            v.tensor_tensor(gate_raw, gate_sgn, gate_abs, ALU.mult).then_inc(pro_v, 1)
            dve.wait_ge(pro_mm, 5)
            ps_mod = small[:, 0, 0:16 * B].rearrange("p (k b) -> p k b", b=B)
            for l in range(LAYERS):
                v.tensor_copy(modT[:, 8 * l:8 * l + 4, :], ps_mod[:, 8 * l:8 * l + 4, :]).then_inc(v_chain, 1)
                v.tensor_scalar_add(modT[:, 8 * l + 4:8 * l + 8, :], ps_mod[:, 8 * l + 4:8 * l + 8, :], 1.0)\
                    .then_inc(v_chain, 1)
            dve.wait_ge(pro_v, 7)
            v.memset(x_res[:, 1], 0.0).then_inc(v_chain, 1)
            v.memset(ctxT[:], 0.0).then_inc(ctx_ready, 1)
            v.memset(ctx_ps[:], 0.0).then_inc(v_chain, 1)
            v.memset(mx[:], 3.0 * NEG).then_inc(v_chain, 1)
            dve.wait_ge(v_chain, 13)
            v.memset(hT[:, :, 0:1], 0.0).then_inc(pro_v, 1)
            CHAIN0 = 13
            chain = [0]

            def link(at, ins):
                chain[0] += 1
                ins.then_inc(v_chain, 1)
                before = {"first": 0, "loop": V_CHAIN[0], "last": V_CHAIN[0] + PAIRS * V_CHAIN[1]}[at.section]
                count = CHAIN0 + before + chain[0]
                dve.wait_ge(v_chain, at.it * V_CHAIN[1] + count if at.section == "loop" else count)

            def layernorm(at, slot, unit, which, n):
                stream, layer = UNITS[unit]
                own = x_res[:, stream]
                if n == 0:
                    if which:
                        for k in range(1, 4):
                            wait_emptied(dve, at, at.turns["proj", unit, k])
                    elif layer:
                        dve.wait_ge(y_added, at.now("y"))
                    else:
                        dve.wait_ge(x_loaded[stream], at.now(f"x_{stream}", 0, 16))
                    b = at.batch(unit, slot, which == 1)
                    settle(dve)
                    cols = modT[:, 8 * layer:8 * layer + 8, b:b + 1] if isinstance(b, int) else \
                        modT[:, 8 * layer:8 * layer + 8, bass.ds(b, 1)]
                    v.tensor_copy(modc[:, which], cols.rearrange("p k o -> p (k o)")).then_inc(modc_ready, 1)
                if n < 2:
                    for t in range(4 * n, 4 * n + 3):
                        v.bn_stats(stats[:, t, :], own[:, t, :])
                    link(at, v.bn_stats(stats[:, 4 * n + 3, :], own[:, 4 * n + 3, :]))
                elif n == 2:
                    settle(dve)
                    for t in range(NT - 1):
                        v.bn_aggr(mv[:, t, :], stats[:, t, :])
                    link(at, v.bn_aggr(mv[:, NT - 1, :], stats[:, NT - 1, :]))
                    link(at, v.tensor_scalar_add(ve[:], mv[:, :, 1], EPS))
                    link(at, v.tensor_scalar(tmp[:].bitcast(i32), ve[:].bitcast(i32), 1, None, ALU.logical_shift_right))
                    link(at, v.tensor_scalar(rstd[:].bitcast(i32), tmp[:].bitcast(i32), -1.0, float(0x5F3759DF),
                                             ALU.mult, ALU.add))
                    for _ in range(3):
                        link(at, v.tensor_tensor(tmp[:], rstd[:], rstd[:], ALU.mult))
                        link(at, v.tensor_tensor(tmp[:], tmp[:], ve[:], ALU.mult))
                        link(at, v.tensor_scalar(tmp[:], tmp[:], -0.5, 1.5, ALU.mult, ALU.add))
                        link(at, v.tensor_tensor(rstd[:], rstd[:], tmp[:], ALU.mult))
                    link(at, v.scalar_tensor_tensor(out=nmr[:], in0=mv[:, :, 0], scalar=-1.0, in1=rstd[:],
                                                    op0=ALU.mult, op1=ALU.mult))
                else:
                    for t in range(4 * (n - 3), 4 * (n - 3) + 4):
                        last = v.tensor_scalar(xn[:, t, :], own[:, t, :], rstd[:, t:t + 1], nmr[:, t:t + 1],
                                               ALU.mult, ALU.add)
                    if n == 4:
                        last.then_inc(xn_ready, 1)

            def step(at, slot, item):
                kind, unit = item[0], item[1]
                stream, layer = UNITS[unit] if unit < 4 else (0, 0)
                if kind in ("rows", "proj", "rope", "y"):
                    bank, emptied = big[:, at.slot(), :], freed[at.slot()]
                if kind == "max":
                    _, _, g, h, qt, blk = item
                    held = small[:, at.small()]
                    to = mx[:, g % 2, h * NT + qt, blk:blk + 1]
                    dve.wait_ge(s_filled, at.now("max", 1))
                    if qt // 4 > blk:
                        ins = v.reduce_max(to, held, AX)
                    else:
                        width = (qt % 4 + 1) * P
                        settle(dve)
                        ins = v.tensor_tensor_reduce(
                            out=held[:, 0:width], in0=held[:, 0:width], in1=mask[:, BANK - width:],
                            scale=1.0, scalar=3.0 * NEG, op0=ALU.add, op1=ALU.max, accum_out=to)
                    ins.then_inc(s_freed, 1)
                    if (h, qt, blk) == (GH - 1, NT - 1, BLOCKS - 1):
                        dve.wait_ge(s_freed, at.now("max", 1 + RING))
                        v.tensor_tensor(mxc[:, g % 2, :], mx[:, g % 2, :, 0], mx[:, g % 2, :, 1], ALU.max)\
                            .then_inc(max_ready, 1)
                elif kind == "rows":
                    g = item[2]
                    wait_filled(dve, at)
                    turned = bank[0:GH * NT, 0:P]
                    link(at, v.tensor_scalar(m_hi[:, g % 2, :], turned, -1.0 / MAX_UNIT, None, ALU.mult))
                    v.scalar_tensor_tensor(out=m_lo[:, g % 2, :], in0=turned, scalar=-1.0 / MAX_UNIT,
                                           in1=m_hi[:, g % 2, :], op0=ALU.mult, op1=ALU.subtract).then_inc(emptied, 1)
                elif kind == "norm":
                    _, g, blk = item
                    n = slot * NG * BLOCKS + g * BLOCKS + blk
                    dve.wait_ge(ctx_saved, at.loops(4 * NG * BLOCKS) + n + 1 + BLOCKS)
                    v.transpose(ctx_b[:], ctx_u[:, blk]).then_inc(u_read, 1)
                    dve.wait_ge(u_read, at.loops(4 * NG * BLOCKS) + n + 1 + BLOCKS)
                    own = ctx_b[:].rearrange("p (c r) -> p c r", r=32)
                    pair = ctx_n[:, blk].rearrange("p (c r) -> p c r", r=32)
                    link(at, v.reciprocal(own[:, :, DH:DH + 1], own[:, :, DH:DH + 1]))
                    link(at, v.tensor_tensor(pair[:, :, DH * (g % 2):DH * (g % 2 + 1)], own[:, :, 0:DH],
                                             own[:, :, DH:DH + 1].broadcast_to([P, BANK // 32, DH]), ALU.mult))
                    if g % 2:
                        v.transpose(ctxT[:, g // 2, blk * BANK:(blk + 1) * BANK], ctx_n[:, blk]).then_inc(ctx_ready, 1)
                elif kind == "proj":
                    n = item[2]
                    if layer == 0 and n == 0:
                        dve.wait_ge(biased, at.now("bias"))
                    wait_filled(dve, at)
                    own = x_res[:, stream, 2 * n:2 * n + 2, :]
                    v.tensor_tensor(own, own, bank.rearrange("p (t n) -> p t n", t=2), ALU.add).then_inc(emptied, 1)
                elif kind == "ln":
                    layernorm(at, slot, unit, item[2], item[3])
                elif kind == "mix":
                    _, _, fc, tb = item
                    if (fc, tb) == (0, 0):
                        for a in ((0, 1), (1, 0), (1, 1)):
                            wait_emptied(dve, at, at.turns["turned", unit, 1, *a])
                    to = slice(tb * BANK, (tb + 1) * BANK)
                    link(at, v.tensor_tensor(k_act[:, fc, to], hT[:, fc, 1 + tb * BANK:1 + (tb + 1) * BANK],
                                             hT[:, fc, to], ALU.subtract))
                    for w, mix in enumerate((mix_r, mix_k)):
                        last = v.scalar_tensor_tensor(out=mix[:, fc, to], in0=k_act[:, fc, to],
                                                      scalar=mu_c[:, w, fc:fc + 1], in1=hT[:, fc, to],
                                                      op0=ALU.mult, op1=ALU.add)
                    last.then_inc(mixed, 1)
                elif kind == "square":
                    _, _, ft, tb = item
                    wait_emptied(dve, at, at.turns["key", unit, ft, tb])
                    own = k_act[:, ft, tb * BANK:(tb + 1) * BANK]
                    v.tensor_tensor(own, own, own, ALU.mult).then_inc(squared, 1)
                elif kind == "y":
                    n = item[2]
                    own = x_res[:, stream, 2 * n:2 * n + 2, :]
                    add = bank.rearrange("p (t n) -> p t n", t=2)
                    if layer and n == 0:
                        dve.wait_ge(biased, at.now("bias"))
                    wait_filled(dve, at)
                    if layer:
                        v.tensor_tensor(own, own, add, ALU.add).then_inc(emptied, 1)
                        wait_emptied(dve, at, at.turn())
                        dve.sem_inc(y_added, 1)
                    else:
                        prod = v_prod[:, 2 * n:2 * n + 2]
                        v.scalar_tensor_tensor(out=prod, in0=r_gate[:, 2 * n:2 * n + 2, :], scalar=1.0, in1=add,
                                               op0=ALU.add, op1=ALU.mult).then_inc(emptied, 1)
                        wait_emptied(dve, at, at.turn())
                        v.scalar_tensor_tensor(out=own, in0=prod, scalar=0.5, in1=own, op0=ALU.mult, op1=ALU.add)\
                            .then_inc(y_added, 1)
                elif kind == "rope":
                    _, _, ft, w, tb = item
                    if (ft, w, tb) == (0, 0, 0):
                        dve.wait_ge(tables_loaded, at.now("tables", 0, 32))
                    wait_filled(dve, at)
                    v.tensor_tensor(rope_sin[:, at.own("rope") % 2], bank, sin_sb[:, tb * BANK:(tb + 1) * BANK], ALU.mult)\
                        .then_inc(emptied, 1)
                elif kind == "split":
                    _, _, ft, w, tb = item
                    own = qk32[:, w, tb * BANK:(tb + 1) * BANK]
                    if (w, tb) == (0, 0) and (at.section != "first" or ft):
                        dve.wait_ge(parts_saved, at.now("parts_save", 0, 32))
                    if layer:
                        n = at.own("rope_split")
                        wait_emptied(dve, at, at.turns["rope", unit, ft, w, tb])
                        dve.wait_ge(rope_cos_ready, at.now("rope_split", 1))
                        link(at, v.tensor_tensor(own, rope_cos[:, n % 2], rope_sin[:, n % 2], ALU.add))
                    else:
                        wait_emptied(dve, at, at.turns["qk", unit, ft, w, tb])
                    hi, lo = (parts[:, w, s, tb * BANK:(tb + 1) * BANK] for s in range(2))
                    link(at, v.tensor_copy(hi, own))
                    v.tensor_tensor(lo, own, hi, ALU.subtract).then_inc(split_done, 1)

            at = Place("first")
            for item in FIRST_ITEMS:
                step(at, 3, item)
                at.done(item)
            assert chain[0] == V_CHAIN[0], chain[0]
            chain[0] = 0
            with dve.Fori(0, PAIRS) as it:
                at = Place("loop", it)
                for slot, item in LOOP_ITEMS:
                    step(at, slot, item)
                    at.done(item)
                assert chain[0] == V_CHAIN[1], chain[0]
            chain[0] = 0
            at = Place("last")
            for item in LAST_ITEMS:
                step(at, 0, item)
                at.done(item)

        @block.tensor
        def _(pe):
            te = nc.tensor
            pe.wait_ge(consts_in, 16 * n_consts)
            pe.wait_ge(consts_set, 3)
            te.matmul(small[0:4, 1, 0:D], lora_a, lora_b, start=True, stop=True).then_inc(pro_mm, 1)
            pe.wait_ge(pro_v, 4)
            te.matmul(small[0:50, 1, D:2 * D], lora_c, lora_1, start=True, stop=True).then_inc(pro_mm, 1)
            pe.wait_ge(pro_v, 5)
            for c in range(FC):
                last = te.matmul(small[:, 2, c * D:(c + 1) * D], lora_2[:, c * P:(c + 1) * P], lora_d,
                                 start=True, stop=True)
            last.then_inc(pro_mm, 1)
            for gi in range(2 * LAYERS):
                l, part = gi // 2, (2, 5)[gi % 2]
                for c in range(FC):
                    last = te.matmul(ctx_ps[0:B, gi // 2, (gi % 2) * D:(gi % 2 + 1) * D], silu_o[:, l, c, :],
                                     wmod_sb[:, l, c, part * D:(part + 1) * D], start=(c == 0), stop=(c == FC - 1))
            last.then_inc(pro_mm, 1)
            for l in range(LAYERS):
                for k, part in enumerate((0, 3, 1, 4)):
                    for fc in range(FC):
                        col = (8 * l + 2 * k + fc) * B
                        for c in range(FC):
                            last = te.matmul(small[:, 0, col:col + B],
                                             wmod_sb[:, l, c, part * D + fc * P:part * D + (fc + 1) * P],
                                             silu_o[:, l, c, :], start=(c == 0), stop=(c == FC - 1))
            last.then_inc(pro_mm, 1)
            pe.wait_ge(pro_v, 8)

            def feature_turn(at, w, rhs, ft, tb):
                wait_bank(pe, at)
                for c in range(FC):
                    last = te.matmul(big[:, at.slot(), :], w[:, c, ft * P:(ft + 1) * P],
                                     rhs[:, c, tb * BANK:(tb + 1) * BANK], start=(c == 0), stop=(c == FC - 1))
                last.then_inc(filled, 1)

            def token_turn(at, lhs, w, n):
                wait_bank(pe, at)
                for t in range(2):
                    for c in range(FC):
                        last = te.matmul(big[:, at.slot(), t * D:(t + 1) * D],
                                         lhs[:, c, (n * 2 + t) * P:(n * 2 + t + 1) * P], w[:, c, :],
                                         start=(c == 0), stop=(c == FC - 1))
                last.then_inc(filled, 1)

            def wait_h(at, unit, which):
                for a in ((0, 1), (1, 0), (1, 1)):
                    wait_emptied(pe, at, at.turns["turned", unit, which, *a])

            def step(at, slot, item):
                kind, unit = item[0], item[1]
                layer = UNITS[unit][1] if unit < 4 else 0
                h_all = hT[:, :, 1:]
                if kind == "max":
                    _, _, g, h, qt, blk = item
                    if (h, qt, blk) == (0, 0, 0) and g % 2 == 0:
                        pe.wait_ge(stacked[g // 2], at.now(f"stack_{g // 2}", 0, 160))
                    pe.wait_ge(s_freed, at.now("max", 1))
                    k0, k1 = blk * BANK, min((blk + 1) * BANK, (qt + 1) * P)
                    te.matmul(small[:, at.small(), 0:k1 - k0], stack_q[:, g * GH + h, qt * P:(qt + 1) * P],
                              stack_k[:, g * GH + h, k0:k1], start=True, stop=True).then_inc(s_filled, 1)
                elif kind == "rows":
                    pe.wait_ge(max_ready, at.now("rows", 1))
                    wait_bank(pe, at)
                    te.transpose(big[0:GH * NT, at.slot(), 0:P], mxc[:, item[2] % 2, :], ident[:]).then_inc(filled, 1)
                elif kind == "score":
                    _, g, blk, kt, q0, heads = item
                    if (blk, kt, heads[0]) == (0, 0, 0):
                        pe.wait_ge(rows_sent[g % 2], at.now(f"rows_{g % 2}", 0, 32))
                    wait_bank(pe, at)
                    for j, h in enumerate(heads):
                        last = te.matmul(big[:, at.slot(), j * (BANK - q0):(j + 1) * (BANK - q0)],
                                         stack_k[:, g * GH + h, kt * P:(kt + 1) * P],
                                         stack_q[:, g * GH + h, blk * BANK + q0:(blk + 1) * BANK], start=True, stop=True)
                    last.then_inc(filled, 1)
                elif kind == "context":
                    _, g, blk, kt, q0 = item
                    n = context_number(slot, g, blk, kt)
                    if kt == 0:
                        pe.wait_ge(ctx_saved, at.loops(4 * NG * BLOCKS) + slot * NG * BLOCKS + g * BLOCKS + blk + 1)
                    if is_diagonal(blk, kt):
                        pe.wait_ge(masked, at.loops(4 * NG * NT) + (slot * NG + g) * NT + kt + 1)
                    else:
                        wait_emptied(pe, at, at.turns["score", g, blk, kt])
                    for h in range(GH):
                        last = te.matmul(ctx_ps[32 * h:32 * h + DH + 1, blk, q0:], v_ones[:, kt, g * GH + h, :],
                                         probs[:, n % RING, h, q0:], start=(kt == 0), stop=(kt == (blk + 1) * 4 - 1))
                    last.then_inc(pv_done, 1)
                elif kind == "proj":
                    if item[2] == 0:
                        pe.wait_ge(scaled, at.now("scale"))
                        pe.wait_ge(ctx_ready, at.now("ctx_ready", 1))
                    token_turn(at, ctxT, w_out, item[2])
                elif kind == "turned":
                    _, _, which, fc, tb = item
                    pe.wait_ge(xn_ready, at.now("normed"))
                    wait_bank(pe, at)
                    for j in range(4):
                        last = te.transpose(big[:, at.slot(), j * P:(j + 1) * P],
                                            xn[:, tb * 4 + j, fc * P:(fc + 1) * P], ident[:])
                    last.then_inc(filled, 1)
                elif kind == "qk":
                    _, _, ft, w, tb = item
                    if (ft, w, tb) == (0, 0, 0):
                        wait_h(at, unit, 0)
                        pe.wait_ge(pre_loaded, at.now("pre_loads", 0, 16))
                    feature_turn(at, w_qkv[:, w], h_all, ft, tb)
                elif kind == "rope":
                    _, _, ft, w, tb = item
                    wait_emptied(pe, at, at.turns["qk", unit, ft, w, tb])
                    wait_bank(pe, at)
                    te.matmul(big[:, at.slot(), :], perm_sb[:], qk32[:, w, tb * BANK:(tb + 1) * BANK],
                              start=True, stop=True).then_inc(filled, 1)
                elif kind == "value":
                    _, _, half, n = item
                    wait_bank(pe, at)
                    for j in range(4):
                        t = n * 4 + j
                        for c in range(FC):
                            last = te.matmul(big[:, at.slot(), j * P:(j + 1) * P], h_all[:, c, t * P:(t + 1) * P],
                                             w_qkv[:, 2, c, half * P:(half + 1) * P], start=(c == 0), stop=(c == FC - 1))
                    last.then_inc(filled, 1)
                elif kind == "gate":
                    if item[2] == 0:
                        pe.wait_ge(mixed, at.now("mix"))
                    token_turn(at, mix_r, w_ffn[:, 0], item[2])
                elif kind == "key":
                    _, _, ft, tb = item
                    feature_turn(at, w_ffn[:, 1], mix_k, ft, tb)
                elif kind == "y":
                    if item[2] == 0:
                        pe.wait_ge(scaled, at.now("scale"))
                        if layer:
                            wait_h(at, unit, 1)
                        else:
                            pe.wait_ge(squared, at.now("square"))
                    token_turn(at, h_all if layer else k_act, w_ffn[:, 2], item[2])

            sections(pe, step)


def shape_constants():
    slopes = (2.0 ** (-8.0 * np.arange(1, H + 1, dtype=np.float32) / np.float32(H))).astype(np.float32)
    pos = np.arange(T, dtype=np.float32)
    rest = (slopes[:, None] * pos[None, :] * np.float32(SCALE)).astype(np.float32)
    alibi = np.zeros((N_ALIBI, H, T), np.float16)
    for n in range(N_ALIBI):
        alibi[n] = rest.astype(np.float16)
        rest = rest - alibi[n].astype(np.float32)
    zero = np.zeros((N_ALIBI, H, T), np.float16)
    one = np.ones((N_ALIBI, H, T), np.float16)
    unit = np.full((N_MAX, H, T), MAX_UNIT, np.float16)
    inv = (1.0 / np.float32(10000.0) ** (np.arange(0, DH, 2, dtype=np.float32) / np.float32(DH))).astype(np.float32)
    freqs = np.outer(pos, inv).astype(np.float32)
    emb = np.concatenate([freqs, freqs], axis=-1)
    cos = np.ascontiguousarray(np.tile(np.cos(emb).astype(np.float32).T, (HPT, 1)))
    sin = np.ascontiguousarray(np.tile(np.sin(emb).astype(np.float32).T, (HPT, 1)))
    perm = np.zeros((P, P), np.float32)
    for h in range(HPT):
        for d in range(DH // 2):
            perm[h * DH + d + DH // 2, h * DH + d] = -1.0
            perm[h * DH + d, h * DH + d + DH // 2] = 1.0
    return alibi, zero, one, unit, perm, cos, sin


def context_rows(w):
    return w.reshape(NG // 2, 2, GH, DH, -1).transpose(0, 2, 1, 3, 4).reshape(H * DH, -1)


def kernel(**inputs):
    import concourse.bacc as bacc
    from concourse.bass_utils import run_bass_kernel_spmd

    a = {k: np.asarray(v) for k, v in inputs.items()}
    alibi, zero, one, unit, perm, cos, sin = shape_constants()
    arrays = {
        "x": a["L0_attn_x"],
        "c0": a["L0_c"].T, "c1": a["L1_c"].T, "wmod0": a["L0_wmod"], "wmod1": a["L1_wmod"],
        "wqkv": np.stack([np.stack([a["L0_attn_W_query"], a["L0_attn_W_key"], a["L0_attn_W_value"]]),
                          np.stack([a["L1_attn_Wq"].T, a["L1_attn_Wk"].T, a["L1_attn_Wv"].T])]),
        "wout": np.stack([context_rows(a["L0_attn_W_proj"]), context_rows(a["L1_attn_Wo"].T)]),
        "bias": np.stack([a["L0_attn_b_proj"], a["L1_ffn_b"]]),
        "wffn": np.stack([a["L0_ffn_W_r"].T, a["L0_ffn_W_k"].T, a["L0_ffn_W_v"].T]),
        "mu": np.stack([a["L0_ffn_mu_r"], a["L0_ffn_mu_k"]]).reshape(2 * FC, P).T,
        "down_t": a["L1_ffn_lora_down"].T, "down_aux": a["L1_ffn_down_aux"],
        "up_t": a["L1_ffn_lora_up"].T, "up_aux_t": a["L1_ffn_up_aux"].T,
        "wbase": a["L1_ffn_W"].T,
        "perm": perm, "cos": cos, "sin": sin,
        "alibi": alibi, "zero": zero, "one": one, "unit": unit,
    }
    arrays = {k: np.ascontiguousarray(v) for k, v in arrays.items()}
    nc = bacc.Bacc("TRN2", target_bir_lowering=False, num_devices=1)
    ap = {k: nc.dram_tensor(k, v.shape, mybir.dt.from_np(v.dtype), kind="ExternalInput").ap() for k, v in arrays.items()}
    out = nc.dram_tensor("out", (B, T, D), mybir.dt.float32, kind="ExternalOutput").ap()
    adaln_program(nc, ap["x"], ap["c0"], ap["c1"], ap["wmod0"], ap["wmod1"], ap["wqkv"], ap["wout"], ap["bias"],
                  ap["wffn"], ap["mu"], (ap["down_t"], ap["down_aux"], ap["up_t"], ap["up_aux_t"]), ap["wbase"],
                  (ap["perm"], ap["cos"], ap["sin"]), (ap["alibi"], ap["zero"], ap["one"], ap["unit"]), out)
    r = run_bass_kernel_spmd(nc, [arrays], core_ids=[0])
    return r.results[0]["out"]
```

```python
import numpy as np

import concourse.bass as bass
from concourse import mybir
from contextlib import ExitStack

B, T, D = 8, 1024, 256
H, DH = 16, 16
P = 128
NT = T // P
FC = D // P
GH = 4
NG = H // GH
HPT = P // DH
BANK = 512
RING = 4
SMALL = 3
HELD = 4
BLOCKS = T // BANK
HH = H // 2
LAYERS = 2
EPS = 1e-5
SCALE = 0.25
NEG = -1e30

Q_PARTS = (0, 0, 1, 1)
K_PARTS = (0, 1, 0, 1)
ROW_ALIBI = len(Q_PARTS) * DH
N_ALIBI = 3
ROW_MAX = ROW_ALIBI + N_ALIBI
N_MAX = 2
MAX_UNIT = 64.0
K_USED = ROW_MAX + N_MAX


UNITS = ((0, 0), (1, 0), (0, 1), (1, 1))
PAIRS = B // 2


def block_tiles(blk):
    return [(kt, max(0, kt * P - blk * BANK)) for kt in range((blk + 1) * BANK // P)]


def is_diagonal(blk, kt):
    return kt >= blk * (BANK // P)


def score_turns(blk):
    out = []
    for kt, q0 in block_tiles(blk):
        n = {512: 1, 384: 1, 256: 2, 128: 4}[BANK - q0]
        out += [(kt, q0, tuple(range(h, h + n))) for h in range(0, GH, n)]
    return out


def attention_items():
    turns = [(g, blk, *t) for g in range(NG) for blk in range(BLOCKS) for t in score_turns(blk)]
    after = {}
    items, at = [], 0.0
    for n in range(len(turns) + LAG + 6):
        if n < len(turns):
            g, blk, kt, q0, heads = turns[n]
            items.append((at, ("score", g, blk, kt, q0, heads)))
            at += len(heads) * (BANK - q0)
            if n + 1 == len(turns) or turns[n + 1][:3] != turns[n][:3]:
                if is_diagonal(blk, kt):
                    items.append((at, ("mask", g, blk, kt, q0)))
                after.setdefault(n + LAG, []).append(("context", g, blk, kt, q0))
                if kt == (blk + 1) * BANK // P - 1:
                    after.setdefault(n + LAG + 1, []).append(("save", g, blk))
                    for part in range(4 if g % 2 else 3):
                        after.setdefault(n + LAG + 2 + part, []).append(("norm", g, blk, part))
        for item in after.get(n, []):
            items.append((at, item))
            if item[0] == "context":
                at += 4 * (BANK - item[4])
    return [(p / at, i) for p, i in items]


LAG = 4
QK_LAGS = (0.0, 1.2, 2.6, 2.8, 4.7)


MAX_BANKS = (((0, 0, 0), (2, 0, P)), ((1, 0, 0), (5, 1, 2 * P)), ((3, 0, 0),), ((4, 0, 0),), ((4, 1, 0), (6, 1, P)),
             ((5, 0, 0),), ((6, 0, 0),), ((7, 0, 0),), ((7, 1, 0),))


def piece_width(qt, blk):
    return BANK if qt // 4 > blk else (qt % 4 + 1) * P


def max_steps():
    steps = []
    for g in range(NG):
        own = [("max", g, h, pieces) for h in range(GH) for pieces in MAX_BANKS]
        if g:
            own[1:1] = [("join", g - 1)]
            own.insert(3, ("rows", g - 1))
        steps += own
    return steps + [("join", NG - 1), ("rows", NG - 1)]


MAX_STEPS = max_steps()
MAX_N = len([s for s in MAX_STEPS if s[0] == "max"]) // NG
LEAD = MAX_N + 11


def step_cost(step):
    if step[0] != "max":
        return {"rows": 350, "join": 60}[step[0]]
    return sum(80 + piece_width(qt, blk) for qt, blk, _ in step[3])


def max_items(slot):
    steps = [(slot, s) for s in MAX_STEPS[LEAD:]] + [((slot + 1) % 4, s) for s in MAX_STEPS[:LEAD]]
    n = len(MAX_STEPS) - LEAD
    steps[n - 2:n + 4] = [steps[n], steps[n - 2], *steps[n + 1:n + 4], steps[n - 1]]
    total = sum(step_cost(s) for _, s in steps)
    items, at = [], 0.0
    for unit, s in steps:
        items.append((at / total, (s[0], unit, *s[1:])))
        at += step_cost(s)
    return items


def spread(start, end, items):
    return [(start + (end - start) * n / len(items), i) for n, i in enumerate(items)]


def y_items(unit, start, end):
    y, a = ([(kind, unit, n) for n in range(4)] for kind in ("y", "y_add"))
    return spread(start, end, [y[0], y[1], a[0], y[2], a[1], y[3], a[2], a[3]])


def staggered(start, end, kinds, lags):
    items = [(n + lag, kind, n) for kind, lag in zip(kinds, lags) for n in range(4)]
    return spread(start, end, [(kind, n) for _, kind, n in sorted(items, key=lambda x: x[0])])


LN_STEPS = 33


def post_items(unit, at):
    layer = UNITS[unit][1]
    proj = [("proj", unit, n) for n in range(4)]
    norm = [("ln", unit, 1, n) for n in range(LN_STEPS)]
    turned = [("turned", unit, 1, fc, tb) for fc in range(FC) for tb in range(2)]
    items = [(0.002, ("scale", unit, 0))]
    if layer == 0:
        items += spread(0.004, 0.06, [("bias", unit, n) for n in range(4)])
    items += spread(at["proj"][0], at["proj"][1], proj)
    items += spread(at["ln2"][0], at["ln2"][1], norm)
    items += spread(at["turn2"][0], at["turn2"][1], turned)
    items += [(at["turn2"][0], ("scale", unit, 1))]
    if layer == 0:
        items += spread(*at["mix"], [("mix", unit, fc, tb, part) for tb in range(2) for part in range(3)
                                     for fc in range(FC)])
        k, s = ([(kind, unit, ft, tb) for ft in range(FC) for tb in range(2)] for kind in ("key", "square"))
        items += spread(*at["ffn"], [("gate", unit, n) for n in range(4)] + [*k[:3], s[0], k[3], *s[1:]])
        items += y_items(unit, *at["y0"])
        items += [(at["y0"][1] + 0.002, ("post_loads", (unit + 1) % 4))]
    else:
        items += spread(*at["bias2"], [("bias", unit, n) for n in range(4)])
        items += y_items(unit, *at["y1"])
        step = (at["y1"][1] - at["y1"][0]) / 4
        for n in range(4):
            done = at["y1"][0] + (n + 1.8) * step
            items += [(done, ("store", unit, n)), (done + 0.7 * step, ("x_load", (unit + 2) % 4, n))]
        items += [(at["y1"][1] + 0.002, ("post_loads", (unit + 1) % 4))]
    return items


def pre_items(unit, at):
    layer = UNITS[unit][1]
    items = [(at["v1"] + 0.01, ("pre_loads", unit))]
    items += spread(*at["ln1"], [("ln", unit, 0, n) for n in range(LN_STEPS)])
    items += spread(*at["turn1"], [("turned", unit, 0, fc, tb) for fc in range(FC) for tb in range(2)])
    kinds, lags = (("qk", "rope", "sum", "hi", "split"), QK_LAGS) if layer else (("qk", "hi", "split"), QK_LAGS[:3])
    for ft in range(FC):
        items += [(p, (kind, unit, ft, n // 2, n % 2)) for p, (kind, n) in staggered(*at[f"qk{ft}"], kinds, lags)]
        items += [(at[f"qk{ft}"][1] + 0.01, ("parts_save", unit, ft))]
    items += [(at["stack0"], ("stack_load", unit, 0))]
    items += spread(*at["v0"], [("value", unit, 0, n) for n in range(2)])
    return items


LIGHT = {"v1": 0.0500,
         "proj": (0.0850, 0.1350),
         "ln2": (0.1435, 0.1800),
         "turn2": (0.1992, 0.2242),
         "bias2": (0.2000, 0.2400),
         "y1": (0.2420, 0.3220),
         "ln1": (0.3719, 0.4300),
         "turn1": (0.4450, 0.4750),
         "qk0": (0.4900, 0.6100),
         "stack0": 0.6269,
         "qk1": (0.6704, 0.8004),
         "v0": (0.8245, 0.8585)}
HEAVY = {"v1": 0.0443,
         "proj": (0.0575, 0.1075),
         "ln2": (0.1291, 0.1860),
         "turn2": (0.2010, 0.2260),
         "mix": (0.2360, 0.2508),
         "ffn": (0.2765, 0.3765),
         "y0": (0.3983, 0.4383),
         "ln1": (0.4561, 0.4911),
         "turn1": (0.5021, 0.5271),
         "qk0": (0.5418, 0.6318),
         "stack0": 0.6568,
         "qk1": (0.6666, 0.7866),
         "v0": (0.7922, 0.8630)}


def pe_cost(item):
    return {"proj": 1720, "gate": 1720, "y": 1720, "key": 1720, "qk": 1720, "value": 1740, "rope": 860,
            "turned": 440}.get(item[0], 0)


def dve_cost(item):
    if item[0] == "ln":
        return 335 if item[3] < 8 else 600 if item[3] == 8 else 77 if item[3] < 25 else 0
    return {"proj": 600, "y": 600, "y_add": 500, "rope": 600, "mix": 400}.get(item[0], 0)


def give_way(items, dense, cost, own, share):
    marks = sorted((p, cost(i)) for p, i in dense)
    total = own + share * sum(c for _, c in marks)
    out, n, passed = [], 0, 0.0
    for p, i in items:
        while n < len(marks) and p * total - passed > own * marks[n][0]:
            passed += share * marks[n][1]
            n += 1
        out.append((max(marks[n - 1][0] if n else 0.0, (p * total - passed) / own), i))
    return out


def merge(others, steps):
    out, steps, pe, dve, ends = [], list(steps), 0.0, 0.0, [0.0] * SMALL
    for p, i in others:
        while steps and (steps[0][0] <= p - WINDOW or (steps[0][0] <= p + WINDOW and dve <= pe + SLACK)):
            if steps[0][1][0] == "rows" and out and out[-1][0] == "half" and i == out[-1][2]:
                break
            if steps[0][1][0] == "rows" and any(o[0] == "half" and o[2] == i for o in out[-4:]):
                break
            step = steps.pop(0)[1]
            if step[0] == "max":
                pe = max(pe, ends[-SMALL]) + step_columns(step) * 0.42
                dve = max(dve, pe + 100) + step_columns(step) * 1.04 + 70
                ends.append(dve)
            else:
                dve += 350
            out.append(step)
        if i[0] == "score":
            pe += len(i[5]) * (BANK - i[4]) * 0.42
        elif i[0] == "context":
            pe += 70 + (BANK - i[4]) * 1.67
        elif i[0] == "norm":
            dve += (600, 100, 300, 600)[i[3]]
        elif i[0] == "half":
            pe += pe_cost(i[2]) / 2
        else:
            pe += pe_cost(i) / (2 if i[0] in HALVED else 1)
            cost = dve_cost(i)
            if cost:
                dve = max(dve, pe) + cost
        out.append(i)
    return out + [step for _, step in steps]


def step_columns(step):
    return sum(piece_width(qt, blk) for qt, blk, _ in step[4])


WINDOW, SLACK = 0.0070, 10.0
HALVED = ("proj", "gate", "y", "key", "qk", "value")


def slot_items(slot):
    before, behind = (slot - 1) % 4, (slot + 1) % 4
    at = LIGHT if UNITS[before][1] else HEAVY
    dense = [(0.03, ("stack_load", slot, 1))] + spread(at["v1"], at["v1"] + 0.01, [("value", slot, 1, n) for n in range(2)])
    dense += post_items(before, at) + pre_items(behind, at)
    others = sorted(give_way(attention_items(), dense, pe_cost, 158000.0, WAY[0]) + dense, key=lambda x: x[0])
    split = []
    for p, i in others:
        if i[0] in HALVED:
            split.append((p, ("half", i[1], i)))
        split.append((p, i))
    out = merge(split, give_way(max_items(slot), dense, dve_cost, 110000.0, WAY[1]))
    for g in range(1, NG):
        assert out.index(("rows", slot, g)) < [i[:4] for i in out].index(("score", g, 0, 0)), g
    return out


WAY = (-0.80, -0.41)
FIRST_ITEMS = [i for _, i in sorted([x for x in pre_items(0, LIGHT)], key=lambda x: x[0])] + \
    [(s[0], 0, *s[1:]) for s in MAX_STEPS[:LEAD]]
FIRST_ITEMS = [("x_load", 0, n) for n in range(4)] + FIRST_ITEMS[:1] + [("spill", 0), ("post_loads", 3)] + FIRST_ITEMS[1:]
assert FIRST_ITEMS[4] == ("pre_loads", 0)
LOOP_ITEMS = [(slot, i) for slot in range(4) for i in slot_items(slot)]
LAST_ITEMS = [i for _, i in sorted(post_items(3, LIGHT), key=lambda x: x[0]) if i[0] not in ("post_loads", "x_load")]

TURN_KINDS = ("score", "rows", "proj", "turned", "gate", "key", "y", "qk", "rope", "value")


def events(item):
    kind = item[0]
    e = {"item": 1, kind: 1}
    if kind in TURN_KINDS:
        e["turn"] = 1
    if kind == "rows":
        e[f"rows_{item[2] % 2}"] = 1
    if kind == "stack_load":
        e[f"stack_{item[2]}"] = 1
    if kind == "ln" and item[3] == LN_STEPS - 1:
        e["normed"] = 1
    if kind == "norm" and item[3] == 3:
        e["ctx_ready"] = 1
    if kind == "mix" and item[4] != 1:
        e["diff" if item[4] == 0 else "mixed"] = 1
    if kind == "x_load":
        e[f"x_{UNITS[item[1]][0]}"] = 1
    if kind == "ln" and item[2:] == (0, 0) and UNITS[item[1]][1]:
        e["tables"] = 1
    return e


def totals(items):
    sums = {}
    for i in items:
        for k, n in events(i).items():
            sums[k] = sums.get(k, 0) + n
    return sums


FIRST = totals(FIRST_ITEMS)
EACH = totals([i for _, i in LOOP_ITEMS])
assert EACH["turn"] % RING == 0 and EACH["max"] % SMALL == 0 and EACH["context"] % HELD == 0
V_CHAIN = (18, 216)
CONTEXTS = NG * sum(len(block_tiles(blk)) for blk in range(BLOCKS))


def context_number(slot, g, blk, kt):
    return slot * CONTEXTS + g * (CONTEXTS // NG) + (len(block_tiles(0)) if blk else 0) + kt


class Place:

    def __init__(self, section, it=None):
        self.section, self.it, self.counts, self.turns = section, it, {}, {}

    def base(self, kind, first=None, each=None):
        first = FIRST.get(kind, 0) if first is None else first
        each = EACH.get(kind, 0) if each is None else each
        return {"first": lambda: 0, "loop": lambda: self.it * each + first,
                "last": lambda: PAIRS * each + first}[self.section]()

    def own(self, kind):
        return self.counts.get(kind, 0)

    def now(self, kind, more=0, unit=1):
        if self.section == "loop":
            return self.it * (EACH.get(kind, 0) * unit) + (FIRST.get(kind, 0) + self.own(kind) + more) * unit
        return (self.base(kind) + self.own(kind) + more) * unit

    def turn(self):
        return self.own("turn")

    def slot(self, turn=None):
        turn = self.turn() if turn is None else turn
        return (turn if self.section == "first" else FIRST["turn"] + turn) % RING

    def uses(self, turn):
        if self.section == "first":
            return turn // RING
        n = (FIRST["turn"] + turn) // RING
        return (self.it * (EACH["turn"] // RING) if self.section == "loop" else PAIRS * (EACH["turn"] // RING)) + n

    def small(self):
        return (self.own("max") + (0 if self.section == "first" else FIRST["max"])) % SMALL

    def loops(self, each):
        return self.it * each

    def done(self, item):
        if item[0] in TURN_KINDS:
            self.turns[item] = self.turn()
            if item[0] == "score":
                self.turns[item[:4]] = self.turn()
        for k, n in events(item).items():
            self.counts[k] = self.counts.get(k, 0) + n

    def batch(self, unit, slot, post):
        if self.section != "loop":
            return B - 1 if post else 0
        stream = UNITS[unit][0]
        if post and slot == 0:
            return (self.it * 2 + (B - 1)) % B
        if not post and slot == 3:
            return (self.it * 2 + 2) % B
        return self.it * 2 + stream


def adaln_program(nc, x, c0, c1, wmod0, wmod1, wqkv, wout, bias, wffn, mu, lora, wbase, rope, rows_c, out):
    f32, f16, bf16, i32 = mybir.dt.float32, mybir.dt.float16, mybir.dt.bfloat16, mybir.dt.int32
    ALU = mybir.AluOpType
    ACT = mybir.ActivationFunctionType
    AX = mybir.AxisListType.X
    down_t, down_aux, up_t, up_aux_t = lora
    perm, cos, sin = rope
    alibi_rows, zero_rows, one_rows, unit_rows = rows_c

    parts_dram = nc.dram_tensor("parts_dram", (2, FC, 2, P, T), f16, kind="Internal").ap()
    gate_dram = nc.dram_tensor("gate_dram", (B, LAYERS, 2 * D), f32, kind="Internal").ap()
    weff_dram = nc.dram_tensor("weff_dram", (P, FC * D), f32, kind="Internal").ap()

    ctx = ExitStack()
    with ctx:
        def sb(name, shape, dt=f32):
            return ctx.enter_context(nc.sbuf_tensor(name, shape, dt))

        def sem(name):
            return ctx.enter_context(nc.semaphore(name))

        x_res = sb("x_res", [P, 2, NT, D])
        xn = sb("xn", [P, NT, D])
        hT = sb("hT", [P, FC, T + 1])
        stack_q = sb("stack_q", [P, H, T], f16)
        stack_k = sb("stack_k", [P, H, T], f16)
        v_ones = sb("v_ones", [P, NT, H, DH + 1])
        probs = sb("probs", [P, HELD, GH, BANK])
        ctx_u = sb("ctx_u", [P, BANK])
        ctx_b = sb("ctx_b", [P, BANK])
        ctx_n = sb("ctx_n", [P, BLOCKS, BANK])
        ctxT = sb("ctxT", [P, NG // 2, T])
        region = sb("region", [P, 8 * T])
        mask = sb("mask", [P, BANK], bf16)
        mx = sb("mx", [P, 2, GH * NT, 2])
        mxc = sb("mxc", [P, 2, GH * NT])
        m_hi = sb("m_hi", [GH * NT, 2, P], f16)
        m_lo = sb("m_lo", [GH * NT, 2, P], f16)
        w_qkv = sb("w_qkv", [P, 3, FC, D])
        w_out = sb("w_out", [P, NG // 2, D])
        w_ffn = sb("w_ffn", [P, 3, FC, D])
        gates = sb("gates", [P, 2, D])
        bias_bc = sb("bias_bc", [P, D])
        modT = sb("modT", [P, 16, B])
        modc = sb("modc", [P, 2, 8])
        mu_c = sb("mu_c", [P, 2, FC])
        ident = sb("ident", [P, P])
        perm_sb = sb("perm_sb", [P, P])
        stats = sb("stats", [P, NT, 6])
        mv = sb("mv", [P, NT, 2])
        ve = sb("ve", [P, NT])
        rstd = sb("rstd", [P, NT])
        tmp = sb("tmp", [P, NT])
        nmr = sb("nmr", [P, NT])
        qk32 = region[:, 0:2 * T].rearrange("p (w t) -> p w t", w=2)
        parts = region[:, 2 * T:4 * T].bitcast(f16).rearrange("p (w s t) -> p w s t", w=2, s=2)
        rope_sin = region[:, 4 * T:5 * T].rearrange("p (a t) -> p a t", a=2)
        rope_cos = region[:, 5 * T:6 * T].rearrange("p (a t) -> p a t", a=2)
        cos_sb = region[:, 6 * T:7 * T]
        sin_sb = region[:, 7 * T:8 * T]
        mix_r = region[:, 0:2 * T].rearrange("p (f t) -> p f t", f=FC)
        mix_k = region[:, 2 * T:4 * T].rearrange("p (f t) -> p f t", f=FC)
        k_act = region[:, 4 * T:6 * T].rearrange("p (f t) -> p f t", f=FC)
        r_gate = region[:, 6 * T:8 * T].rearrange("p (t n) -> p t n", t=NT)
        v_prod = xn
        wmod_sb = region[:, 0:6 * T].rearrange("p (l c n) -> p l c n", l=2, c=FC)
        silu_in = ctx_b[:, 0:32].rearrange("p (l c b) -> p l c b", l=2, c=FC)
        silu_e = ctx_b[:, 32:64].rearrange("p (l c b) -> p l c b", l=2, c=FC)
        silu_o = ctx_b[:, 64:96].rearrange("p (l c b) -> p l c b", l=2, c=FC)
        gate_raw = probs[0:B, 0, 0:2, :].rearrange("b t n -> b (t n)")
        gate_neg = probs[0:B, 0, 2:4, :].rearrange("b t n -> b (t n)")
        gate_abs = probs[0:B, 1, 0:2, :].rearrange("b t n -> b (t n)")
        gate_sgn = probs[0:B, 1, 2:4, :].rearrange("b t n -> b (t n)")
        room = xn[:].rearrange("p t n -> p (t n)")
        lora_a = room[0:100, 0:4]
        lora_b = room[0:100, 8:8 + D]
        lora_c = room[0:4, 272:322]
        lora_d = room[0:50, 328:328 + D]
        lora_1 = room[0:4, 592:592 + D]
        lora_2 = room[0:50, 856:856 + D]
        w_lin = w_ffn[:, 2]

        big = ctx.enter_context(nc.psum_tensor("big", [P, RING, BANK], f32))
        ctx_ps = ctx.enter_context(nc.psum_tensor("ctx_ps", [P, BANK], f32))
        small = ctx.enter_context(nc.psum_tensor("small", [P, SMALL, BANK], f32))

        consts_in = sem("consts_in")
        consts_set = sem("consts_set")
        stacks_clear = sem("stacks_clear")
        silu_exp = sem("silu_exp")
        pro_mm = sem("pro_mm")
        pro_v = sem("pro_v")
        gates_out = sem("gates_out")
        rows_in = sem("rows_in")
        x_loaded = [sem("x_loaded_0"), sem("x_loaded_1")]
        post_loaded = sem("post_loaded")
        pre_loaded = sem("pre_loaded")
        tables_loaded = sem("tables_loaded")
        filled = sem("filled")
        freed = [sem(f"freed_{i}") for i in range(RING)]
        s_filled = sem("s_filled")
        s_freed = sem("s_freed")
        xn_ready = sem("xn_ready")
        factors_ready = sem("factors_ready")
        hi_ready = sem("hi_ready")
        sum_done = sem("sum_done")
        diff_ready = sem("diff_ready")
        modc_ready = sem("modc_ready")
        split_done = sem("split_done")
        parts_saved = sem("parts_saved")
        stacked = [sem("stacked_0"), sem("stacked_1")]
        rope_cos_ready = sem("rope_cos_ready")
        max_ready = sem("max_ready")
        rows_sent = [sem("rows_sent_0"), sem("rows_sent_1")]
        masked = sem("masked")
        pv_done = sem("pv_done")
        ctx_saved = sem("ctx_saved")
        u_read = sem("u_read")
        ctx_ready = sem("ctx_ready")
        scaled = sem("scaled")
        bias_gated = sem("bias_gated")
        biased = sem("biased")
        mixed = sem("mixed")
        squared = sem("squared")
        y_added = sem("y_added")
        stored = sem("stored")
        v_chain = sem("v_chain")
        g_chain = sem("g_chain")
        waits_taken = sem("waits_taken")

        def settle(eng):
            eng.sem_inc(waits_taken, 1)

        def wait_filled(eng, at):
            eng.wait_ge(filled, at.now("turn", 1))

        def wait_bank(eng, at):
            eng.wait_ge(freed[at.slot()], at.uses(at.turn()) + 1)

        def wait_emptied(eng, at, turn):
            eng.wait_ge(freed[at.slot(turn)], at.uses(turn) + 2)

        def wait_all_emptied(eng, at, turns):
            for turn in {at.slot(t): t for t in sorted(turns)}.values():
                wait_emptied(eng, at, turn)

        def sections(eng, step):
            at = Place("first")
            for item in FIRST_ITEMS:
                step(at, 3, item)
                at.done(item)
            with eng.Fori(0, PAIRS) as it:
                at = Place("loop", it)
                for slot, item in LOOP_ITEMS:
                    step(at, slot, item)
                    at.done(item)
            at = Place("last")
            for item in LAST_ITEMS:
                step(at, 0, item)
                at.done(item)

        n_consts = 11
        block = ctx.enter_context(nc.Block())

        @block.sync
        def _(sp):
            def load(dst, src):
                sp.dma_start(dst, src).then_inc(consts_in, 16)

            for l, (c, w) in enumerate(((c0, wmod0), (c1, wmod1))):
                load(silu_in[:, l], c.rearrange("(c p) b -> p c b", p=P))
                load(wmod_sb[:, l], w.rearrange("(c p) n -> p c n", p=P))
            load(w_lin, wbase.rearrange("(c p) n -> p c n", p=P))
            load(lora_a, down_t)
            load(lora_b, down_aux)
            load(lora_c, up_t)
            load(lora_d, up_aux_t)
            load(mu_c[:].rearrange("p w c -> p (w c)"), mu)
            load(perm_sb[:], perm)

            def step(at, slot, item):
                kind, unit = item[0], item[1]
                stream, layer = UNITS[unit] if unit < 4 else (0, 0)
                if kind == "spill":
                    sp.wait_ge(pro_v, 7)
                    sp.dma_start(gate_dram.rearrange("b l n -> b (l n)"), gate_raw).then_inc(gates_out, 16)
                    sp.dma_start(weff_dram, w_lin.rearrange("p c n -> p (c n)")).then_inc(gates_out, 16)
                    sp.wait_ge(gates_out, 32)
                    sp.wait_ge(pro_v, 8)
                    sp.wait_ge(stacks_clear, 2)
                    for half in range(2):
                        heads = slice(half * HH, (half + 1) * HH)
                        sp.dma_start(stack_q[ROW_ALIBI:ROW_MAX, heads], one_rows[:, heads]).then_inc(rows_in, 16)
                        sp.dma_start(stack_k[ROW_MAX:K_USED, heads], unit_rows[:, heads]).then_inc(rows_in, 16)
                    sp.wait_ge(rows_in, 64)
                elif kind == "post_loads":
                    if at.section != "first":
                        sp.wait_ge(y_added, at.now("y_add"))
                        settle(sp)
                    b = at.it * 2 + stream if at.section == "loop" else B - 1
                    src = wout[layer].rearrange("(g p) n -> p g n", p=P)
                    sp.dma_start(w_out[:], src).then_inc(post_loaded, 16)
                    if layer == 0:
                        sp.dma_start(w_ffn[:], wffn.rearrange("w (c p) n -> p w c n", p=P)).then_inc(post_loaded, 16)
                    else:
                        sp.dma_start(w_lin, weff_dram.rearrange("p (c n) -> p c n", c=FC)).then_inc(post_loaded, 16)
                    gsrc = gate_dram[b:b + 1, layer] if isinstance(b, int) else \
                        gate_dram[bass.ds(b, 1), layer]
                    sp.dma_start(gates[:].rearrange("p g n -> p (g n)"), gsrc.broadcast_to([P, 2 * D]))\
                        .then_inc(post_loaded, 16)
                    sp.dma_start(bias_bc[:], bias[layer:layer + 1, :].broadcast_to([P, D])).then_inc(post_loaded, 16)
                elif kind == "pre_loads":
                    if at.section != "first":
                        sp.wait_ge(filled, at.now("turn"))
                    sp.dma_start(w_qkv[:], wqkv[layer].rearrange("w (c p) n -> p w c n", p=P)).then_inc(pre_loaded, 16)
                elif kind == "ln" and item[2] == 0 and item[3] == 0 and layer == 1:
                    sp.wait_ge(y_added, at.now("y_add"))
                    sp.dma_start(cos_sb, cos).then_inc(tables_loaded, 16)
                    sp.dma_start(sin_sb, sin).then_inc(tables_loaded, 16)
                elif kind == "parts_save":
                    ft = item[2]
                    sp.wait_ge(split_done, at.now("split"))
                    for w in range(2):
                        sp.dma_start(parts_dram[w, ft].rearrange("s p t -> p s t"), parts[:, w])\
                            .then_inc(parts_saved, 16)
                elif kind == "stack_load":
                    half = item[2]
                    if at.section != "first":
                        sp.wait_ge(filled, at.now("turn"))
                        settle(sp)
                    sp.wait_ge(parts_saved, at.now("parts_save", 0, 32))
                    for w, (stack, order) in enumerate(((stack_q, Q_PARTS), (stack_k, K_PARTS))):
                        for r, s in enumerate(order):
                            sp.dma_start(stack[r * DH:(r + 1) * DH, half * HH:(half + 1) * HH, :],
                                         parts_dram[w, half, s].rearrange("(h d) t -> d h t", d=DH))\
                                .then_inc(stacked[half], 16)
                    heads = slice(half * HH, (half + 1) * HH)
                    sp.dma_start(stack_k[ROW_ALIBI:ROW_MAX, heads], (zero_rows if layer else alibi_rows)[:, heads])\
                        .then_inc(stacked[half], 16)
                    sp.dma_start(stack_q[ROW_MAX:K_USED, heads], zero_rows[0:N_MAX, heads]).then_inc(stacked[half], 16)
                elif kind == "rows":
                    g = item[2]
                    wait_emptied(sp, at, at.turn())
                    for r, m in enumerate((m_hi, m_lo)):
                        sp.dma_start(stack_q[ROW_MAX + r:ROW_MAX + r + 1, g * GH:(g + 1) * GH, :]
                                     .rearrange("r h (q t) -> r (h q) t", t=P), m[:, g % 2, :])\
                            .then_inc(rows_sent[g % 2], 16)
                elif kind == "store":
                    sp.wait_ge(y_added, at.now("y_add"))
                    settle(sp)
                    b = at.batch(unit, slot, True)
                    n = item[2]
                    dst = out[b] if isinstance(b, int) else out[bass.ds(b, 1)].rearrange("o n d -> (o n) d")
                    sp.dma_start(dst.rearrange("(t p) n -> p t n", p=P)[:, 2 * n:2 * n + 2],
                                 x_res[:, stream, 2 * n:2 * n + 2]).then_inc(stored, 16)
                elif kind == "x_load":
                    if at.section != "first":
                        sp.wait_ge(stored, at.now("store", 0, 16))
                        settle(sp)
                    b = at.batch(unit, slot, False)
                    src = x[b] if isinstance(b, int) else x[bass.ds(b, 1)].rearrange("o n d -> (o n) d")
                    n = item[2]
                    sp.dma_start(x_res[:, stream, 2 * n:2 * n + 2],
                                 src.rearrange("(t p) n -> p t n", p=P)[:, 2 * n:2 * n + 2])\
                        .then_inc(x_loaded[stream], 16)

            sections(sp, step)
            sp.wait_ge(stored, 16 * 4 * (PAIRS * 2 + 1))
            sp.wait_ge(x_loaded[0], 16 * 4 * (PAIRS + 1))

        @block.gpsimd
        def _(pool):
            g = nc.gpsimd
            g.memset(ident[:], 0.0).then_inc(g_chain, 1)
            g.memset(mask[:], 0.0).then_inc(g_chain, 1)
            g.memset(v_ones[:], 1.0).then_inc(consts_set, 1)
            g.memset(x_res[:, 1], 0.0).then_inc(consts_set, 1)
            g.memset(ctxT[:], 0.0).then_inc(ctx_ready, 1)
            pool.wait_ge(g_chain, 2)
            g.affine_select(out=ident[:], in_=ident[:], compare_op=ALU.not_equal, fill=1.0, base=0,
                            pattern=[[-1, P]], channel_multiplier=1).then_inc(consts_set, 1)
            g.affine_select(out=mask[:, BANK - P:], in_=mask[:, BANK - P:], compare_op=ALU.is_ge, fill=NEG, base=0,
                            pattern=[[-1, P]], channel_multiplier=1).then_inc(consts_set, 1)
            pool.wait_ge(consts_set, 4)
            pool.wait_ge(ctx_ready, 1)
            g.memset(stack_k[P // 2:], 0.0).then_inc(stacks_clear, 1)
            pool.wait_ge(stacks_clear, 2)
            pool.wait_ge(consts_in, 16 * n_consts)

            def step(at, slot, item):
                kind, unit = item[0], item[1]
                if kind == "mask":
                    _, g_, blk, kt, q0 = item
                    wait_emptied(pool, at, at.turns["score", g_, blk, kt])
                    settle(pool)
                    diag = probs[:, context_number(slot, g_, blk, kt) % HELD, :, q0:q0 + P]
                    g.affine_select(out=diag, in_=diag, compare_op=ALU.is_ge, fill=0.0, base=0,
                                    pattern=[[0, GH], [1, P]], channel_multiplier=-1).then_inc(masked, 1)
                elif kind == "scale" and item[2] == 0:
                    layer = UNITS[unit][1]
                    pool.wait_ge(post_loaded, at.now("post_loads", 0, 64))
                    g.tensor_tensor(w_out[:], w_out[:], gates[:, 0:1, :].broadcast_to([P, NG // 2, D]), ALU.mult)\
                        .then_inc(scaled, 1)
                    g.tensor_tensor(bias_bc[:], bias_bc[:], gates[:, layer], ALU.mult).then_inc(bias_gated, 1)
                elif kind == "scale":
                    g.tensor_tensor(w_ffn[:, 2], w_ffn[:, 2], gates[:, 1:2, :].broadcast_to([P, FC, D]), ALU.mult)\
                        .then_inc(scaled, 1)
                elif kind == "bias":
                    stream, layer = UNITS[unit]
                    n = item[2]
                    if n == 0:
                        pool.wait_ge(bias_gated, at.now("post_loads", 0))
                        pool.wait_ge(xn_ready, at.now("normed"))
                    own = x_res[:, stream, 2 * n:2 * n + 2]
                    g.tensor_tensor(own, own, bias_bc[:].rearrange("p (o n) -> p o n", o=1).broadcast_to([P, 2, D]),
                                    ALU.add).then_inc(biased, 1)
                elif kind == "mix" and item[4] == 0:
                    _, _, fc, tb, _ = item
                    if (fc, tb) == (0, 0):
                        wait_all_emptied(pool, at, [at.turns["turned", unit, 1, c, k] for c in range(FC) for k in range(2)])
                    to = slice(tb * BANK, (tb + 1) * BANK)
                    g.tensor_tensor(k_act[:, fc, to], hT[:, fc, 1 + tb * BANK:1 + (tb + 1) * BANK], hT[:, fc, to],
                                    ALU.subtract).then_inc(diff_ready, 1)
                elif kind == "square":
                    _, _, ft, tb = item
                    wait_emptied(pool, at, at.turns["key", unit, ft, tb])
                    own = k_act[:, ft, tb * BANK:(tb + 1) * BANK]
                    g.tensor_tensor(own, own, own, ALU.mult).then_inc(squared, 1)
                elif kind == "sum":
                    _, _, ft, w, tb = item
                    own, n = qk32[:, w, tb * BANK:(tb + 1) * BANK], at.own("sum")
                    wait_emptied(pool, at, at.turns["rope", unit, ft, w, tb])
                    pool.wait_ge(rope_cos_ready, at.now("sum", 1))
                    g.tensor_tensor(own, rope_cos[:, n % 2], rope_sin[:, n % 2], ALU.add).then_inc(sum_done, 1)
                elif kind == "split":
                    _, _, ft, w, tb = item
                    own = qk32[:, w, tb * BANK:(tb + 1) * BANK]
                    pool.wait_ge(hi_ready, at.now("split", 1))
                    hi, lo = (parts[:, w, s, tb * BANK:(tb + 1) * BANK] for s in range(2))
                    g.tensor_tensor(lo, own, hi, ALU.subtract).then_inc(split_done, 1)
                elif kind == "rope":
                    _, _, ft, w, tb = item
                    if ft == 0 and w == 0 and tb == 0:
                        pool.wait_ge(tables_loaded, at.now("tables", 0, 32))
                    n = at.own("rope")
                    wait_emptied(pool, at, at.turns["qk", unit, ft, w, tb])
                    if at.own("sum"):
                        pool.wait_ge(sum_done, at.now("sum"))
                    else:
                        pool.wait_ge(split_done, at.now("split"))
                    g.tensor_tensor(rope_cos[:, n % 2], qk32[:, w, tb * BANK:(tb + 1) * BANK],
                                    cos_sb[:, tb * BANK:(tb + 1) * BANK], ALU.mult).then_inc(rope_cos_ready, 1)

            sections(pool, step)

        @block.scalar
        def _(act):
            s = nc.scalar
            act.wait_ge(consts_in, 16 * n_consts)
            s.activation(silu_e, silu_in, ACT.Exp, scale=-1.0).then_inc(silu_exp, 1)

            def step(at, slot, item):
                kind, unit = item[0], item[1]
                layer = UNITS[unit][1] if unit < 4 else 0
                if kind in TURN_KINDS and kind not in ("rows", "proj", "rope", "y"):
                    bank, emptied = big[:, at.slot(), :], freed[at.slot()]
                if kind == "score":
                    _, g, blk, kt, q0, heads = item
                    n = context_number(slot, g, blk, kt)
                    if heads[0] == 0:
                        act.wait_ge(pv_done, at.loops(4 * CONTEXTS) + n + 1)
                    wait_filled(act, at)
                    width = BANK - q0
                    s.activation(probs[:, n % HELD, heads[0]:heads[-1] + 1, q0:],
                                 bank[:, 0:len(heads) * width].rearrange("p (h q) -> p h q", h=len(heads)), ACT.Exp)\
                        .then_inc(emptied, 1)
                elif kind == "save":
                    _, g, blk = item
                    n = slot * NG * BLOCKS + g * BLOCKS + blk
                    act.wait_ge(pv_done, at.loops(4 * CONTEXTS) + context_number(slot, g, blk, (blk + 1) * 4 - 1) + 1 + HELD)
                    act.wait_ge(u_read, at.loops(4 * NG * BLOCKS) + n + 1)
                    s.activation(ctx_u[:], ctx_ps[:], ACT.Copy).then_inc(ctx_saved, 1)
                elif kind == "turned":
                    _, _, which, fc, tb = item
                    act.wait_ge(modc_ready, at.now("normed"))
                    wait_filled(act, at)
                    col = which * 2 + fc
                    s.activation(hT[:, fc, 1 + tb * BANK:1 + (tb + 1) * BANK], bank, ACT.Identity,
                                 scale=modc[:, which, col + 4:col + 5], bias=modc[:, which, col:col + 1])\
                        .then_inc(emptied, 1)
                elif kind == "qk":
                    _, _, ft, w, tb = item
                    if at.section != "first" or at.own("split"):
                        act.wait_ge(split_done, at.now("split"))
                    wait_filled(act, at)
                    s.activation(qk32[:, w, tb * BANK:(tb + 1) * BANK], bank, ACT.Copy, scale=SCALE if w == 0 else 1.0)\
                        .then_inc(emptied, 1)
                elif kind == "hi":
                    _, _, ft, w, tb = item
                    if layer:
                        act.wait_ge(sum_done, at.now("sum"))
                    else:
                        wait_emptied(act, at, at.turns["qk", unit, ft, w, tb])
                    if at.section != "first" or ft:
                        act.wait_ge(parts_saved, at.now("parts_save", 0, 32))
                    s.activation(parts[:, w, 0, tb * BANK:(tb + 1) * BANK], qk32[:, w, tb * BANK:(tb + 1) * BANK],
                                 ACT.Copy).then_inc(hi_ready, 1)
                elif kind == "ln" and item[3] >= LN_STEPS - NT:
                    t = item[3] - (LN_STEPS - NT)
                    if t == 0:
                        act.wait_ge(factors_ready, at.now("normed", 1))
                    ins = s.activation(xn[:, t, :], x_res[:, UNITS[unit][0], t, :], ACT.Identity,
                                       scale=rstd[:, t:t + 1], bias=nmr[:, t:t + 1])
                    if t == NT - 1:
                        ins.then_inc(xn_ready, 1)
                elif kind == "value":
                    _, _, half, n = item
                    wait_filled(act, at)
                    s.activation(v_ones[:, n * 4:(n + 1) * 4, half * HH:(half + 1) * HH, 0:DH],
                                 bank.rearrange("p (t h d) -> p t h d", t=4, h=HH), ACT.Copy).then_inc(emptied, 1)
                elif kind == "gate":
                    n = item[2]
                    wait_filled(act, at)
                    s.activation(r_gate[:, 2 * n:2 * n + 2, :], bank.rearrange("p (t n) -> p t n", t=2), ACT.Tanh,
                                 scale=0.5).then_inc(emptied, 1)
                elif kind == "key":
                    _, _, ft, tb = item
                    wait_filled(act, at)
                    s.activation(k_act[:, ft, tb * BANK:(tb + 1) * BANK], bank, ACT.Relu).then_inc(emptied, 1)

            sections(act, step)

        @block.vector
        def _(dve):
            v = nc.vector
            v.memset(stack_q[P // 2:], 0.0).then_inc(stacks_clear, 1)
            for bank in freed:
                dve.sem_inc(bank, 1)
            dve.sem_inc(s_freed, SMALL)
            dve.sem_inc(pv_done, HELD)
            dve.sem_inc(ctx_saved, 1)
            dve.sem_inc(u_read, 1)
            dve.wait_ge(consts_in, 16 * n_consts)
            dve.wait_ge(silu_exp, 1)
            v.tensor_scalar_add(silu_e, silu_e, 1.0).then_inc(pro_v, 1)
            dve.wait_ge(pro_v, 1)
            v.reciprocal(silu_e, silu_e).then_inc(pro_v, 1)
            dve.wait_ge(pro_v, 2)
            v.tensor_tensor(silu_o, silu_in, silu_e, ALU.mult).then_inc(pro_v, 1)
            dve.wait_ge(pro_mm, 1)
            v.tensor_copy(lora_1, small[0:4, 1, 0:D]).then_inc(pro_v, 1)
            dve.wait_ge(pro_mm, 2)
            v.tensor_copy(lora_2, small[0:50, 1, D:2 * D]).then_inc(pro_v, 1)
            dve.wait_ge(pro_mm, 3)
            v.tensor_tensor(w_lin, w_lin, small[:, 2, :].rearrange("p (c n) -> p c n", c=FC), ALU.add)\
                .then_inc(pro_v, 1)
            dve.wait_ge(pro_mm, 4)
            v.tensor_copy(gate_raw[:, 0:2 * D], ctx_ps[0:B]).then_inc(v_chain, 1)
            v.tensor_copy(gate_raw[:, 2 * D:], big[0:B, 0, :]).then_inc(v_chain, 1)
            dve.wait_ge(v_chain, 2)
            v.tensor_scalar(gate_neg, gate_raw, -1.0, None, ALU.mult).then_inc(v_chain, 1)
            v.tensor_scalar(gate_sgn, gate_raw, 0.0, 2.0, ALU.is_ge, ALU.mult).then_inc(v_chain, 1)
            dve.wait_ge(v_chain, 4)
            v.tensor_tensor(gate_abs, gate_raw, gate_neg, ALU.max).then_inc(v_chain, 1)
            dve.wait_ge(v_chain, 5)
            v.tensor_scalar(gate_sgn, gate_sgn, -1.0, None, ALU.add).then_inc(v_chain, 1)
            v.tensor_scalar(gate_abs, gate_abs, 0.25, None, ALU.max).then_inc(v_chain, 1)
            dve.wait_ge(v_chain, 7)
            v.tensor_tensor(gate_raw, gate_sgn, gate_abs, ALU.mult).then_inc(pro_v, 1)
            dve.wait_ge(pro_mm, 5)
            ps_mod = small[:, 0, 0:16 * B].rearrange("p (k b) -> p k b", b=B)
            for l in range(LAYERS):
                v.tensor_copy(modT[:, 8 * l:8 * l + 4, :], ps_mod[:, 8 * l:8 * l + 4, :]).then_inc(v_chain, 1)
                v.tensor_scalar_add(modT[:, 8 * l + 4:8 * l + 8, :], ps_mod[:, 8 * l + 4:8 * l + 8, :], 1.0)\
                    .then_inc(v_chain, 1)
            dve.wait_ge(pro_v, 7)
            dve.wait_ge(consts_set, 4)
            v.memset(ctx_ps[:], 0.0).then_inc(v_chain, 1)
            v.memset(mx[:], 3.0 * NEG).then_inc(v_chain, 1)
            dve.wait_ge(v_chain, 13)
            v.memset(hT[:, :, 0:1], 0.0).then_inc(pro_v, 1)
            CHAIN0 = 13
            chain = [0]

            def link(at, ins):
                mark(ins)
                linked(at)

            def mark(ins):
                chain[0] += 1
                ins.then_inc(v_chain, 1)

            def linked(at):
                before = {"first": 0, "loop": V_CHAIN[0], "last": V_CHAIN[0] + PAIRS * V_CHAIN[1]}[at.section]
                count = CHAIN0 + before + chain[0]
                dve.wait_ge(v_chain, at.it * V_CHAIN[1] + count if at.section == "loop" else count)

            def layernorm(at, slot, unit, which, n):
                stream, layer = UNITS[unit]
                own = x_res[:, stream]
                if n == 0:
                    if which:
                        wait_all_emptied(dve, at, [at.turns["proj", unit, k] for k in range(4)])
                    elif layer:
                        dve.wait_ge(y_added, at.now("y_add"))
                    else:
                        dve.wait_ge(x_loaded[stream], at.now(f"x_{stream}", 0, 16))
                    b = at.batch(unit, slot, which == 1)
                    settle(dve)
                    cols = modT[:, 8 * layer:8 * layer + 8, b:b + 1] if isinstance(b, int) else \
                        modT[:, 8 * layer:8 * layer + 8, bass.ds(b, 1)]
                    v.tensor_copy(modc[:, which], cols.rearrange("p k o -> p (k o)")).then_inc(modc_ready, 1)
                if n == 0 and (at.section != "first"):
                    dve.wait_ge(xn_ready, at.now("normed"))
                if n < NT:
                    ins = v.bn_stats(stats[:, n, :], own[:, n, :])
                    if n == NT - 1:
                        mark(ins)
                    return
                if n >= LN_STEPS - NT:
                    return
                linked(at)
                n -= NT
                if n == 0:
                    settle(dve)
                    for t in range(NT - 1):
                        v.bn_aggr(mv[:, t, :], stats[:, t, :])
                    mark(v.bn_aggr(mv[:, NT - 1, :], stats[:, NT - 1, :]))
                elif n == 1:
                    mark(v.tensor_scalar_add(ve[:], mv[:, :, 1], EPS))
                elif n == 2:
                    mark(v.tensor_scalar(tmp[:].bitcast(i32), ve[:].bitcast(i32), 1, None, ALU.logical_shift_right))
                elif n == 3:
                    mark(v.tensor_scalar(rstd[:].bitcast(i32), tmp[:].bitcast(i32), -1.0, float(0x5F3759DF),
                                         ALU.mult, ALU.add))
                elif n == 16:
                    v.scalar_tensor_tensor(out=nmr[:], in0=mv[:, :, 0], scalar=-1.0, in1=rstd[:],
                                           op0=ALU.mult, op1=ALU.mult).then_inc(factors_ready, 1)
                elif n % 4 == 0:
                    mark(v.tensor_tensor(tmp[:], rstd[:], rstd[:], ALU.mult))
                elif n % 4 == 1:
                    mark(v.tensor_tensor(tmp[:], tmp[:], ve[:], ALU.mult))
                elif n % 4 == 2:
                    mark(v.tensor_scalar(tmp[:], tmp[:], -0.5, 1.5, ALU.mult, ALU.add))
                else:
                    mark(v.tensor_tensor(rstd[:], rstd[:], tmp[:], ALU.mult))

            def step(at, slot, item):
                kind, unit = item[0], item[1]
                stream, layer = UNITS[unit] if unit < 4 else (0, 0)
                if kind in ("rows", "proj", "rope", "y"):
                    bank, emptied = big[:, at.slot(), :], freed[at.slot()]
                if kind == "max":
                    _, _, g, h, pieces = item
                    dve.wait_ge(s_filled, at.now("max", 1))
                    for n, (qt, blk, col) in enumerate(pieces):
                        width = piece_width(qt, blk)
                        held = small[:, at.small(), col:col + width]
                        to = mx[:, g % 2, h * NT + qt, blk:blk + 1]
                        if qt // 4 > blk:
                            ins = v.reduce_max(to, held, AX)
                        else:
                            if n == 0:
                                settle(dve)
                            ins = v.tensor_tensor_reduce(
                                out=held, in0=held, in1=mask[:, BANK - width:],
                                scale=1.0, scalar=3.0 * NEG, op0=ALU.add, op1=ALU.max, accum_out=to)
                    ins.then_inc(s_freed, 1)
                elif kind == "join":
                    g = item[2]
                    dve.wait_ge(s_freed, at.now("max", SMALL))
                    v.tensor_tensor(mxc[:, g % 2, :], mx[:, g % 2, :, 0], mx[:, g % 2, :, 1], ALU.max)\
                        .then_inc(max_ready, 1)
                elif kind == "rows":
                    g = item[2]
                    wait_filled(dve, at)
                    turned = bank[0:GH * NT, 0:P]
                    link(at, v.tensor_scalar(m_hi[:, g % 2, :], turned, -1.0 / MAX_UNIT, None, ALU.mult))
                    v.scalar_tensor_tensor(out=m_lo[:, g % 2, :], in0=turned, scalar=-1.0 / MAX_UNIT,
                                           in1=m_hi[:, g % 2, :], op0=ALU.mult, op1=ALU.subtract).then_inc(emptied, 1)
                elif kind == "norm":
                    _, g, blk, part = item
                    n = at.loops(4 * NG * BLOCKS) + slot * NG * BLOCKS + g * BLOCKS + blk + 2
                    own = ctx_b[:].rearrange("p (c r) -> p c r", r=32)
                    pair = ctx_n[:, blk].rearrange("p (c r) -> p c r", r=32)
                    if part == 0:
                        dve.wait_ge(ctx_saved, n)
                        v.transpose(ctx_b[:], ctx_u[:]).then_inc(u_read, 1)
                    elif part == 1:
                        dve.wait_ge(u_read, n)
                        mark(v.reciprocal(own[:, :, DH:DH + 1], own[:, :, DH:DH + 1]))
                    elif part == 2:
                        linked(at)
                        mark(v.tensor_tensor(pair[:, :, DH * (g % 2):DH * (g % 2 + 1)], own[:, :, 0:DH],
                                             own[:, :, DH:DH + 1].broadcast_to([P, BANK // 32, DH]), ALU.mult))
                    else:
                        linked(at)
                        v.transpose(ctxT[:, g // 2, blk * BANK:(blk + 1) * BANK], ctx_n[:, blk]).then_inc(ctx_ready, 1)
                elif kind == "proj":
                    n = item[2]
                    if layer == 0 and n == 0:
                        dve.wait_ge(biased, at.now("bias"))
                    wait_filled(dve, at)
                    own = x_res[:, stream, 2 * n:2 * n + 2, :]
                    v.tensor_tensor(own, own, bank.rearrange("p (t n) -> p t n", t=2), ALU.add).then_inc(emptied, 1)
                elif kind == "ln":
                    layernorm(at, slot, unit, item[2], item[3])
                elif kind == "mix":
                    _, _, fc, tb, part = item
                    to = slice(tb * BANK, (tb + 1) * BANK)
                    if part:
                        if part == 1:
                            dve.wait_ge(diff_ready, at.now("diff"))
                        last = v.scalar_tensor_tensor(out=(mix_r, mix_k)[part - 1][:, fc, to], in0=k_act[:, fc, to],
                                                      scalar=mu_c[:, part - 1, fc:fc + 1], in1=hT[:, fc, to],
                                                      op0=ALU.mult, op1=ALU.add)
                        if part == 2:
                            last.then_inc(mixed, 1)
                elif kind == "y":
                    n = item[2]
                    own = x_res[:, stream, 2 * n:2 * n + 2, :]
                    add = bank.rearrange("p (t n) -> p t n", t=2)
                    if layer and n == 0:
                        dve.wait_ge(biased, at.now("bias"))
                    wait_filled(dve, at)
                    if layer:
                        v.tensor_tensor(own, own, add, ALU.add).then_inc(emptied, 1)
                    else:
                        v.scalar_tensor_tensor(out=v_prod[:, 2 * n:2 * n + 2], in0=r_gate[:, 2 * n:2 * n + 2, :],
                                               scalar=1.0, in1=add, op0=ALU.add, op1=ALU.mult).then_inc(emptied, 1)
                elif kind == "y_add":
                    n = item[2]
                    own = x_res[:, stream, 2 * n:2 * n + 2, :]
                    wait_emptied(dve, at, at.turns["y", unit, n])
                    if layer:
                        dve.sem_inc(y_added, 1)
                    else:
                        prod = v_prod[:, 2 * n:2 * n + 2]
                        v.scalar_tensor_tensor(out=own, in0=prod, scalar=0.5, in1=own, op0=ALU.mult, op1=ALU.add)\
                            .then_inc(y_added, 1)
                elif kind == "rope":
                    _, _, ft, w, tb = item
                    if (ft, w, tb) == (0, 0, 0):
                        dve.wait_ge(tables_loaded, at.now("tables", 0, 32))
                    if at.own("sum"):
                        dve.wait_ge(sum_done, at.now("sum"))
                    wait_filled(dve, at)
                    v.tensor_tensor(rope_sin[:, at.own("rope") % 2], bank, sin_sb[:, tb * BANK:(tb + 1) * BANK], ALU.mult)\
                        .then_inc(emptied, 1)
            at = Place("first")
            for item in FIRST_ITEMS:
                step(at, 3, item)
                at.done(item)
            assert chain[0] == V_CHAIN[0], chain[0]
            chain[0] = 0
            with dve.Fori(0, PAIRS) as it:
                at = Place("loop", it)
                for slot, item in LOOP_ITEMS:
                    step(at, slot, item)
                    at.done(item)
                assert chain[0] == V_CHAIN[1], chain[0]
            chain[0] = 0
            at = Place("last")
            for item in LAST_ITEMS:
                step(at, 0, item)
                at.done(item)

        @block.tensor
        def _(pe):
            te = nc.tensor
            pe.wait_ge(consts_in, 16 * n_consts)
            pe.wait_ge(consts_set, 4)
            te.matmul(small[0:4, 1, 0:D], lora_a, lora_b, start=True, stop=True).then_inc(pro_mm, 1)
            pe.wait_ge(pro_v, 4)
            te.matmul(small[0:50, 1, D:2 * D], lora_c, lora_1, start=True, stop=True).then_inc(pro_mm, 1)
            pe.wait_ge(pro_v, 5)
            for c in range(FC):
                last = te.matmul(small[:, 2, c * D:(c + 1) * D], lora_2[:, c * P:(c + 1) * P], lora_d,
                                 start=True, stop=True)
            last.then_inc(pro_mm, 1)
            for gi in range(2 * LAYERS):
                l, part = gi // 2, (2, 5)[gi % 2]
                for c in range(FC):
                    last = te.matmul((ctx_ps[0:B] if l == 0 else big[0:B, 0, :])[:, (gi % 2) * D:(gi % 2 + 1) * D], silu_o[:, l, c, :],
                                     wmod_sb[:, l, c, part * D:(part + 1) * D], start=(c == 0), stop=(c == FC - 1))
            last.then_inc(pro_mm, 1)
            for l in range(LAYERS):
                for k, part in enumerate((0, 3, 1, 4)):
                    for fc in range(FC):
                        col = (8 * l + 2 * k + fc) * B
                        for c in range(FC):
                            last = te.matmul(small[:, 0, col:col + B],
                                             wmod_sb[:, l, c, part * D + fc * P:part * D + (fc + 1) * P],
                                             silu_o[:, l, c, :], start=(c == 0), stop=(c == FC - 1))
            last.then_inc(pro_mm, 1)
            pe.wait_ge(pro_v, 8)

            def halves(first, second):
                return range(0 if first else 1, 2 if second else 1)

            started = set()

            def feature_turn(at, w, rhs, ft, tb, first, second):
                if first:
                    wait_bank(pe, at)
                for c in halves(first, second):
                    last = te.matmul(big[:, at.slot(), :], w[:, c, ft * P:(ft + 1) * P],
                                     rhs[:, c, tb * BANK:(tb + 1) * BANK], start=(c == 0), stop=(c == FC - 1))
                if second:
                    last.then_inc(filled, 1)

            def token_turn(at, lhs, w, n, first, second):
                if first:
                    wait_bank(pe, at)
                for t in halves(first, second):
                    for c in range(FC):
                        last = te.matmul(big[:, at.slot(), t * D:(t + 1) * D],
                                         lhs[:, c, (n * 2 + t) * P:(n * 2 + t + 1) * P], w[:, c, :],
                                         start=(c == 0), stop=(c == FC - 1))
                if second:
                    last.then_inc(filled, 1)

            def wait_h(at, unit, which):
                wait_all_emptied(pe, at, [at.turns["turned", unit, which, fc, tb] for fc in range(FC) for tb in range(2)])
                settle(pe)

            def step(at, slot, item):
                kind, unit = item[0], item[1]
                layer = UNITS[unit][1] if unit < 4 else 0
                h_all = hT[:, :, 1:]
                first, second = True, True
                if kind == "half":
                    item, second = item[2], False
                    kind = item[0]
                    started.add(item)
                elif item in started:
                    first = False
                    started.discard(item)
                if kind == "max":
                    _, _, g, h, pieces = item
                    if (h, pieces) == (0, MAX_BANKS[0]) and g % 2 == 0:
                        pe.wait_ge(stacked[g // 2], at.now(f"stack_{g // 2}", 0, 160))
                    pe.wait_ge(s_freed, at.now("max", 1))
                    for qt, blk, col in pieces:
                        width = piece_width(qt, blk)
                        last = te.matmul(small[:, at.small(), col:col + width],
                                         stack_q[:, g * GH + h, qt * P:(qt + 1) * P],
                                         stack_k[:, g * GH + h, blk * BANK:blk * BANK + width], start=True, stop=True)
                    last.then_inc(s_filled, 1)
                elif kind == "rows":
                    pe.wait_ge(max_ready, at.now("rows", 1))
                    wait_bank(pe, at)
                    te.transpose(big[0:GH * NT, at.slot(), 0:P], mxc[:, item[2] % 2, :], ident[:]).then_inc(filled, 1)
                elif kind == "score":
                    _, g, blk, kt, q0, heads = item
                    if (blk, kt, heads[0]) == (0, 0, 0):
                        pe.wait_ge(rows_sent[g % 2], at.now(f"rows_{g % 2}", 0, 32))
                    wait_bank(pe, at)
                    for j, h in enumerate(heads):
                        last = te.matmul(big[:, at.slot(), j * (BANK - q0):(j + 1) * (BANK - q0)],
                                         stack_k[:, g * GH + h, kt * P:(kt + 1) * P],
                                         stack_q[:, g * GH + h, blk * BANK + q0:(blk + 1) * BANK], start=True, stop=True)
                    last.then_inc(filled, 1)
                elif kind == "context":
                    _, g, blk, kt, q0 = item
                    n = context_number(slot, g, blk, kt)
                    if kt == 0:
                        pe.wait_ge(ctx_saved, at.loops(4 * NG * BLOCKS) + slot * NG * BLOCKS + g * BLOCKS + blk + 1)
                    if is_diagonal(blk, kt):
                        pe.wait_ge(masked, at.loops(4 * NG * NT) + (slot * NG + g) * NT + kt + 1)
                    else:
                        wait_emptied(pe, at, at.turns["score", g, blk, kt])
                    for h in range(GH):
                        last = te.matmul(ctx_ps[32 * h:32 * h + DH + 1, q0:], v_ones[:, kt, g * GH + h, :],
                                         probs[:, n % HELD, h, q0:], start=(kt == 0), stop=(kt == (blk + 1) * 4 - 1))
                    last.then_inc(pv_done, 1)
                elif kind == "proj":
                    if item[2] == 0 and first:
                        pe.wait_ge(scaled, at.now("scale"))
                        pe.wait_ge(ctx_ready, at.now("ctx_ready", 1))
                    token_turn(at, ctxT, w_out, item[2], first, second)
                elif kind == "turned":
                    _, _, which, fc, tb = item
                    pe.wait_ge(xn_ready, at.now("normed"))
                    wait_bank(pe, at)
                    for j in range(4):
                        last = te.transpose(big[:, at.slot(), j * P:(j + 1) * P],
                                            xn[:, tb * 4 + j, fc * P:(fc + 1) * P], ident[:])
                    last.then_inc(filled, 1)
                elif kind == "qk":
                    _, _, ft, w, tb = item
                    if (ft, w, tb) == (0, 0, 0) and first:
                        wait_h(at, unit, 0)
                        pe.wait_ge(pre_loaded, at.now("pre_loads", 0, 16))
                    feature_turn(at, w_qkv[:, w], h_all, ft, tb, first, second)
                elif kind == "rope":
                    _, _, ft, w, tb = item
                    wait_emptied(pe, at, at.turns["qk", unit, ft, w, tb])
                    wait_bank(pe, at)
                    te.matmul(big[:, at.slot(), :], perm_sb[:], qk32[:, w, tb * BANK:(tb + 1) * BANK],
                              start=True, stop=True).then_inc(filled, 1)
                elif kind == "value":
                    _, _, half, n = item
                    if first:
                        wait_bank(pe, at)
                    for j in range(0 if first else 2, 4 if second else 2):
                        t = n * 4 + j
                        for c in range(FC):
                            last = te.matmul(big[:, at.slot(), j * P:(j + 1) * P], h_all[:, c, t * P:(t + 1) * P],
                                             w_qkv[:, 2, c, half * P:(half + 1) * P], start=(c == 0), stop=(c == FC - 1))
                    if second:
                        last.then_inc(filled, 1)
                elif kind == "gate":
                    if item[2] == 0 and first:
                        pe.wait_ge(mixed, at.now("mixed"))
                    token_turn(at, mix_r, w_ffn[:, 0], item[2], first, second)
                elif kind == "key":
                    _, _, ft, tb = item
                    feature_turn(at, w_ffn[:, 1], mix_k, ft, tb, first, second)
                elif kind == "y":
                    if item[2] == 0 and first:
                        pe.wait_ge(scaled, at.now("scale"))
                        if layer:
                            wait_h(at, unit, 1)
                        else:
                            pe.wait_ge(squared, at.now("square"))
                    token_turn(at, h_all if layer else k_act, w_ffn[:, 2], item[2], first, second)

            sections(pe, step)


def shape_constants():
    slopes = (2.0 ** (-8.0 * np.arange(1, H + 1, dtype=np.float32) / np.float32(H))).astype(np.float32)
    pos = np.arange(T, dtype=np.float32)
    rest = (slopes[:, None] * pos[None, :] * np.float32(SCALE)).astype(np.float32)
    alibi = np.zeros((N_ALIBI, H, T), np.float16)
    for n in range(N_ALIBI):
        alibi[n] = rest.astype(np.float16)
        rest = rest - alibi[n].astype(np.float32)
    zero = np.zeros((N_ALIBI, H, T), np.float16)
    one = np.ones((N_ALIBI, H, T), np.float16)
    unit = np.full((N_MAX, H, T), MAX_UNIT, np.float16)
    inv = (1.0 / np.float32(10000.0) ** (np.arange(0, DH, 2, dtype=np.float32) / np.float32(DH))).astype(np.float32)
    freqs = np.outer(pos, inv).astype(np.float32)
    emb = np.concatenate([freqs, freqs], axis=-1)
    cos = np.ascontiguousarray(np.tile(np.cos(emb).astype(np.float32).T, (HPT, 1)))
    sin = np.ascontiguousarray(np.tile(np.sin(emb).astype(np.float32).T, (HPT, 1)))
    perm = np.zeros((P, P), np.float32)
    for h in range(HPT):
        for d in range(DH // 2):
            perm[h * DH + d + DH // 2, h * DH + d] = -1.0
            perm[h * DH + d, h * DH + d + DH // 2] = 1.0
    return alibi, zero, one, unit, perm, cos, sin


def context_rows(w):
    return w.reshape(NG // 2, 2, GH, DH, -1).transpose(0, 2, 1, 3, 4).reshape(H * DH, -1)


def kernel(**inputs):
    import concourse.bacc as bacc
    from concourse.bass_utils import run_bass_kernel_spmd

    a = {k: np.asarray(v) for k, v in inputs.items()}
    alibi, zero, one, unit, perm, cos, sin = shape_constants()
    arrays = {
        "x": a["L0_attn_x"],
        "c0": a["L0_c"].T, "c1": a["L1_c"].T, "wmod0": a["L0_wmod"], "wmod1": a["L1_wmod"],
        "wqkv": np.stack([np.stack([a["L0_attn_W_query"], a["L0_attn_W_key"], a["L0_attn_W_value"]]),
                          np.stack([a["L1_attn_Wq"].T, a["L1_attn_Wk"].T, a["L1_attn_Wv"].T])]),
        "wout": np.stack([context_rows(a["L0_attn_W_proj"]), context_rows(a["L1_attn_Wo"].T)]),
        "bias": np.stack([a["L0_attn_b_proj"], a["L1_ffn_b"]]),
        "wffn": np.stack([a["L0_ffn_W_r"].T, a["L0_ffn_W_k"].T, a["L0_ffn_W_v"].T]),
        "mu": np.stack([a["L0_ffn_mu_r"], a["L0_ffn_mu_k"]]).reshape(2 * FC, P).T,
        "down_t": a["L1_ffn_lora_down"].T, "down_aux": a["L1_ffn_down_aux"],
        "up_t": a["L1_ffn_lora_up"].T, "up_aux_t": a["L1_ffn_up_aux"].T,
        "wbase": a["L1_ffn_W"].T,
        "perm": perm, "cos": cos, "sin": sin,
        "alibi": alibi, "zero": zero, "one": one, "unit": unit,
    }
    arrays = {k: np.ascontiguousarray(v) for k, v in arrays.items()}
    nc = bacc.Bacc("TRN2", target_bir_lowering=False, num_devices=1)
    ap = {k: nc.dram_tensor(k, v.shape, mybir.dt.from_np(v.dtype), kind="ExternalInput").ap() for k, v in arrays.items()}
    out = nc.dram_tensor("out", (B, T, D), mybir.dt.float32, kind="ExternalOutput").ap()
    adaln_program(nc, ap["x"], ap["c0"], ap["c1"], ap["wmod0"], ap["wmod1"], ap["wqkv"], ap["wout"], ap["bias"],
                  ap["wffn"], ap["mu"], (ap["down_t"], ap["down_aux"], ap["up_t"], ap["up_aux_t"]), ap["wbase"],
                  (ap["perm"], ap["cos"], ap["sin"]), (ap["alibi"], ap["zero"], ap["one"], ap["unit"]), out)
    r = run_bass_kernel_spmd(nc, [arrays], core_ids=[0])
    return r.results[0]["out"]
```
